# Optimizing a Trainium2 kernel written in Bass

```python
import numpy as np
import jax
import jax.numpy as jnp

def _softmax(x, axis=-1):
    return jax.nn.softmax(x, axis=axis)

def _gelu(x):
    return jax.nn.gelu(x, approximate=True)

def _silu(x):
    return jax.nn.silu(x)

def _sigmoid(x):
    return jax.nn.sigmoid(x)

def _layernorm(x, axis=-1, eps=1e-05):
    m = jnp.mean(x, axis=axis, keepdims=True)
    v = jnp.var(x, axis=axis, keepdims=True)
    return (x - m) / jnp.sqrt(v + eps)

def _scatter_add(tgt, idx, src, axis=0):
    return tgt.at[idx].add(src)

def _segment_sum(src, seg, n):
    return jax.ops.segment_sum(src, seg, n)
kernel_name = 'mk_metaformer_d1_conv_nchw512_r4_dc0041'

def setup_inputs(seed: int=0):
    np.random.seed(seed)
    _w = jnp.asarray

    def _rec_inputs():
        import jax
        import jax.numpy as jnp
        _gk = jax.random.key(seed)
        x = -0.0002091 + 1 * jax.random.normal(jax.random.fold_in(_gk, 1), (16, 128, 28, 28), jnp.float32)
        return x
    x = _rec_inputs()

    def _L0_conv_setup():
        import jax, jax.numpy as jnp
        import numpy as np
        from jax import lax
        EPS = 1e-05
        DW_THRESH = 4.0
        PW_THRESH = 0.001
        C_IN = 128
        C_OUT = 128

        def _bn(x, g, b, m, v):
            inv = g * lax.rsqrt(v + EPS)
            return x * inv[None, :, None, None] + (b - m * inv)[None, :, None, None]

        def _prune(x, thresh):
            amax = jnp.max(jnp.abs(x), axis=(2, 3), keepdims=True)
            return jnp.where(amax < thresh, jnp.zeros_like(x), x)
        key = jax.random.key(seed)
        ks = jax.random.split(key, 8)
        B, H, W = (16, 28, 28)
        x = jax.random.normal(ks[0], (B, C_IN, H, W), dtype=jnp.float32)
        dw_w = jax.random.normal(ks[1], (C_IN, 1, 3, 3), dtype=jnp.float32) * 0.1
        dw_b = jax.random.normal(ks[2], (C_IN,), dtype=jnp.float32) * 0.1
        bn1_g = jnp.ones((C_IN,), jnp.float32)
        bn1_b = jnp.zeros((C_IN,), jnp.float32)
        bn1_m = jnp.zeros((C_IN,), jnp.float32)
        bn1_v = jnp.ones((C_IN,), jnp.float32)
        pw_w = jax.random.normal(ks[3], (C_OUT, C_IN, 1, 1), dtype=jnp.float32) * 0.05
        pw_b = jax.random.normal(ks[4], (C_OUT,), dtype=jnp.float32) * 0.1
        bn2_g = jnp.ones((C_OUT,), jnp.float32)
        bn2_b = jnp.zeros((C_OUT,), jnp.float32)
        bn2_m = jnp.zeros((C_OUT,), jnp.float32)
        bn2_v = jnp.ones((C_OUT,), jnp.float32)
        return dict(x=x, dw_w=dw_w, dw_b=dw_b, bn1_g=bn1_g, bn1_b=bn1_b, bn1_m=bn1_m, bn1_v=bn1_v, pw_w=pw_w, pw_b=pw_b, bn2_g=bn2_g, bn2_b=bn2_b, bn2_m=bn2_m, bn2_v=bn2_v)
    _L0_conv_all = _L0_conv_setup()
    _L0_conv_in = {k: v for k, v in _L0_conv_all.items() if k in ('dw_w', 'dw_b', 'bn1_g', 'bn1_b', 'bn1_m', 'bn1_v', 'pw_w', 'pw_b', 'bn2_g', 'bn2_b', 'bn2_m', 'bn2_v')}
    del _L0_conv_all

    def _L0_ffn_setup():
        import jax, jax.numpy as jnp
        import numpy as np
        B, T, D = (4, 2048, 128)
        E, F, CAP = (8, 512, 1024)
        key = jax.random.key(seed)
        ks = jax.random.split(key, 6)
        s = 0.02
        return {'x': jax.random.normal(ks[0], (B, T, D), dtype=jnp.float32), 'Wr': jax.random.normal(ks[1], (D, E), dtype=jnp.float32) * s, 'W1': jax.random.normal(ks[2], (E, D, F), dtype=jnp.float32) * s, 'b1': jax.random.normal(ks[3], (E, F), dtype=jnp.float32) * s, 'W2': jax.random.normal(ks[4], (E, F, D), dtype=jnp.float32) * s, 'b2': jax.random.normal(ks[5], (E, D), dtype=jnp.float32) * s}
    _L0_ffn_all = _L0_ffn_setup()
    _L0_ffn_in = {k: v for k, v in _L0_ffn_all.items() if k in ('Wr', 'W1', 'b1', 'W2', 'b2')}
    del _L0_ffn_all
    return {'x': x, 'L0_conv_dw_w': _L0_conv_in['dw_w'], 'L0_conv_dw_b': _L0_conv_in['dw_b'], 'L0_conv_bn1_g': _L0_conv_in['bn1_g'], 'L0_conv_bn1_b': _L0_conv_in['bn1_b'], 'L0_conv_bn1_m': _L0_conv_in['bn1_m'], 'L0_conv_bn1_v': _L0_conv_in['bn1_v'], 'L0_conv_pw_w': _L0_conv_in['pw_w'], 'L0_conv_pw_b': _L0_conv_in['pw_b'], 'L0_conv_bn2_g': _L0_conv_in['bn2_g'], 'L0_conv_bn2_b': _L0_conv_in['bn2_b'], 'L0_conv_bn2_m': _L0_conv_in['bn2_m'], 'L0_conv_bn2_v': _L0_conv_in['bn2_v'], 'L0_ffn_Wr': _L0_ffn_in['Wr'], 'L0_ffn_W1': _L0_ffn_in['W1'], 'L0_ffn_b1': _L0_ffn_in['b1'], 'L0_ffn_W2': _L0_ffn_in['W2'], 'L0_ffn_b2': _L0_ffn_in['b2']}

def reference(x, L0_conv_dw_w, L0_conv_dw_b, L0_conv_bn1_g, L0_conv_bn1_b, L0_conv_bn1_m, L0_conv_bn1_v, L0_conv_pw_w, L0_conv_pw_b, L0_conv_bn2_g, L0_conv_bn2_b, L0_conv_bn2_m, L0_conv_bn2_v, L0_ffn_Wr, L0_ffn_W1, L0_ffn_b1, L0_ffn_W2, L0_ffn_b2):
    import jax
    import jax.numpy as jnp

    def _L0_conv_ref(x, dw_w, dw_b, bn1_g, bn1_b, bn1_m, bn1_v, pw_w, pw_b, bn2_g, bn2_b, bn2_m, bn2_v):
        import jax, jax.numpy as jnp
        import numpy as np
        from jax import lax
        EPS = 1e-05
        DW_THRESH = 4.0
        PW_THRESH = 0.001
        C_IN = 128
        C_OUT = 128

        def _bn(x, g, b, m, v):
            inv = g * lax.rsqrt(v + EPS)
            return x * inv[None, :, None, None] + (b - m * inv)[None, :, None, None]

        def _prune(x, thresh):
            amax = jnp.max(jnp.abs(x), axis=(2, 3), keepdims=True)
            return jnp.where(amax < thresh, jnp.zeros_like(x), x)
        dn = ('NCHW', 'OIHW', 'NCHW')
        h = lax.conv_general_dilated(x, dw_w, window_strides=(1, 1), padding=((1, 1), (1, 1)), feature_group_count=C_IN, dimension_numbers=dn)
        h = h + dw_b[None, :, None, None]
        h = jax.nn.relu(_bn(h, bn1_g, bn1_b, bn1_m, bn1_v))
        h = _prune(h, DW_THRESH)
        h = lax.conv_general_dilated(h, pw_w, window_strides=(1, 1), padding=((0, 0), (0, 0)), dimension_numbers=dn)
        h = h + pw_b[None, :, None, None]
        h = jax.nn.relu(_bn(h, bn2_g, bn2_b, bn2_m, bn2_v))
        h = _prune(h, PW_THRESH)
        return h

    def _L0_ffn_ref(x, Wr, W1, b1, W2, b2):
        import jax, jax.numpy as jnp
        import numpy as np
        B, T, D = (4, 2048, 128)
        E, F, CAP = (8, 512, 1024)
        Bb, Tt, Dd = x.shape
        N = Bb * Tt
        C = min(CAP, N)
        x_flat = x.reshape(N, Dd)
        logits = x_flat @ Wr
        probs = jax.nn.softmax(logits, axis=0)
        vals, idx = jax.lax.top_k(probs.T, C)
        selected = x_flat[idx]
        h = jax.nn.gelu(jnp.einsum('ecd,edf->ecf', selected, W1) + b1[:, None, :], approximate=False)
        out_e = jnp.einsum('ecf,efd->ecd', h, W2) + b2[:, None, :]
        weighted = vals[..., None] * out_e
        output = jnp.zeros_like(x_flat).at[idx.reshape(-1)].add(weighted.reshape(-1, Dd))
        return output.reshape(Bb, Tt, Dd)

    def _gn(v, G=32, eps=1e-05):
        B_, C_, H_, W_ = v.shape
        g = v.reshape(B_, G, C_ // G, H_, W_)
        m = jnp.mean(g, axis=(2, 3, 4), keepdims=True)
        s = jnp.var(g, axis=(2, 3, 4), keepdims=True)
        return ((g - m) / jnp.sqrt(s + eps)).reshape(v.shape)

    def _ln_c(v, eps=1e-06):
        m = jnp.mean(v, axis=1, keepdims=True)
        s = jnp.var(v, axis=1, keepdims=True)
        return (v - m) / jnp.sqrt(s + eps)

    def _ln_t(v, eps=1e-05):
        m = jnp.mean(v, axis=-1, keepdims=True)
        s = jnp.var(v, axis=-1, keepdims=True)
        return (v - m) / jnp.sqrt(s + eps)

    def _to_tokens(v):
        B_, C_, H_, W_ = v.shape
        return v.reshape(B_, C_, H_ * W_).transpose(0, 2, 1)

    def _from_tokens(t, like):
        B_, C_, H_, W_ = like.shape
        return t.transpose(0, 2, 1).reshape(B_, C_, H_, W_)
    x = x + _L0_conv_ref(_ln_c(x), L0_conv_dw_w, L0_conv_dw_b, L0_conv_bn1_g, L0_conv_bn1_b, L0_conv_bn1_m, L0_conv_bn1_v, L0_conv_pw_w, L0_conv_pw_b, L0_conv_bn2_g, L0_conv_bn2_b, L0_conv_bn2_m, L0_conv_bn2_v)
    t = _to_tokens(x)
    t = t + _L0_ffn_ref(_ln_t(t), L0_ffn_Wr, L0_ffn_W1, L0_ffn_b1, L0_ffn_W2, L0_ffn_b2)
    x = _from_tokens(t, x)
    return x

_drawn_inputs = setup_inputs


def setup_inputs(seed=0):
    import zlib

    import numpy as np

    out = dict(_drawn_inputs(seed))
    spreads = {'L0_conv_bn1_g': (1.0, 0.2),
     'L0_conv_bn1_b': (0.0, 0.1),
     'L0_conv_bn1_m': (0.0, 0.1),
     'L0_conv_bn1_v': (1.0, 0.2),
     'L0_conv_bn2_g': (1.0, 0.6),
     'L0_conv_bn2_b': (0.0, 0.1),
     'L0_conv_bn2_m': (0.0, 0.1),
     'L0_conv_bn2_v': (1.0, 0.6)}
    factors = {'L0_ffn_Wr': 64.0,
     'L0_ffn_W1': 64.0,
     'L0_ffn_b1': 64.0,
     'L0_ffn_W2': 64.0,
     'L0_ffn_b2': 64.0}
    for name, (base, spread) in spreads.items():
        noise = np.random.default_rng([zlib.crc32(name.encode()), seed]).standard_normal(out[name].shape)
        drawn = base * np.exp(spread * noise) if base else spread * noise
        out[name] = jnp.asarray(drawn.astype(out[name].dtype))
    for name, factor in factors.items():
        out[name] = (out[name] * factor).astype(out[name].dtype)
    return out
```

```python
from contextlib import ExitStack

import concourse.bass as bass
from concourse import mybir

ALU = mybir.AluOpType
ACT = mybir.ActivationFunctionType
AX_X = mybir.AxisListType.X
F32 = mybir.dt.float32
F16 = mybir.dt.float16
I32 = mybir.dt.int32
U32 = mybir.dt.uint32
ds = bass.ds

B, C, H, W = 16, 128, 28, 28
HW = H * W
P = 112
TPI = HW // P
TILES = B * TPI
N = B * HW
E, F, CAP = 8, 512, 1024
SB = CAP // 128
FT = F // 128
ROW = C + E
HALF = HW // 2
LINES = H // 2
PW = W + 2
HS = CAP // 2
DW_THRESH, PW_THRESH = 4.0, 0.001
BN_EPS, LN_C_EPS, LN_T_EPS = 1e-5, 1e-6, 1e-5

PE_TAPS = 5
TAPS = [(dy, dx) for dy in range(3) for dx in range(3)]
DVE_TAPS = len(TAPS) - PE_TAPS

LOOP_FIRST, LOOP_END, LAST_PAIR = 3, B // 2, B // 2 + 2
SHIFTS = list(range(29, 0, -2)) + [0]
ROUNDS = len(SHIFTS)


def steps(eng, step):
    for pair in range(LOOP_FIRST):
        for u in range(2):
            step(pair, u)
    with eng.Fori(LOOP_FIRST, LOOP_END) as pair:
        for u in range(2):
            step(pair, u)
    for pair in range(LOOP_END, LAST_PAIR):
        for u in range(2):
            step(pair, u)


def image(pair, u, lag):
    o = u - lag
    img, use = pair * 2 + o, pair + o // 2
    active = not isinstance(pair, int) or 0 <= img < B
    return active, img, o % 2, use


def since(number, first):
    return not isinstance(number, int) or number >= first


def build(nc, x, dw_w, dw_b, bn1_g, bn1_b, bn1_m, bn1_v, pw_w, pw_b, bn2_g, bn2_b, bn2_m, bn2_v,
          Wr, W1, b1, W2, b2, out):
    x_d = x.rearrange("b c h w -> c b (h w)")
    out_d = out.rearrange("b c h w -> c b (h w)")
    w1_d = W1.rearrange("e d f -> d e f")
    w2_d = W2.rearrange("e (t p) d -> p e t d", p=128)

    with ExitStack() as ctx:
        def sb(name, shape, dt=F32):
            return ctx.enter_context(nc.sbuf_tensor(name, shape, dt))

        def sem(name):
            return ctx.enter_context(nc.semaphore(name))

        def pair_of(name):
            return [sem(f"{name}{q}") for q in range(2)]

        rows_dram = nc.dram_tensor("token_rows", (N, ROW), F32).ap()
        y_dram = nc.dram_tensor("moe_sum", (N, C), F32).ap()
        rows_t = rows_dram.rearrange("(i t p) c -> p i t c", p=P, t=TPI)
        y_t = y_dram.rearrange("(i t p) c -> p i t c", p=P, t=TPI)

        psA, psB, psC, psD = (ctx.enter_context(nc.psum_tensor(f"ps{n}", [128, 2, 512], F32)) for n in "ABCD")

        ident = sb("ident", [128, 128])
        ones = sb("ones", [128, 128])
        avg = sb("avg", [128, 128])
        before = sb("before", [P, P])
        same_expert = sb("same_expert", [128, 128])
        mod_i = sb("mod_i", [128, 128], I32)
        tile_row = sb("tile_row", [P, P])
        part_i = sb("part_i", [P, 3], I32)
        tile_col = sb("tile_col", [P, 1])
        slot_row = sb("slot_row", [P, CAP])
        slot_col = sb("slot_col", [128, SB])
        bit_table = sb("bit_table", [128, ROUNDS, 4], I32)
        eps_c = sb("eps_c", [128, 1])
        eps_t = sb("eps_t", [128, 1])
        zero_rows = sb("zero_rows", [P, TPI * C])
        prm = sb("prm", [128, 10])
        fold = sb("fold", [128, 12])
        taps_w = sb("taps_w", [128, 9])
        tap_diag = sb("tap_diag", [128, PE_TAPS, 128])
        pw_raw = sb("pw_raw", [128, 128])
        pw_T = sb("pw_T", [128, 128])
        pw_masked = sb("pw_masked", [128, 2, 128])
        wr_raw = sb("wr_raw", [128, E])
        wr_c = sb("wr_c", [128, E])
        b1_raw = sb("b1_raw", [E * FT, 128])
        b1_T = sb("b1_T", [128, E * FT])
        b2_raw = sb("b2_raw", [E, 128])
        b2_T = sb("b2_T", [128, E])
        x_in = sb("x_in", [128, 2, HW])
        x_res = sb("x_res", [128, 2, HW])
        x_pad = sb("x_pad", [128, 2, (H + 2) * PW])
        ln_tok = sb("ln_tok", [P, 2, TPI * C])
        ln_st = sb("ln_st", [P, TPI, 6])
        ln_sm = sb("ln_sm", [P, 7, TPI])
        row_st = sb("row_st", [P, TPI, 6])
        row_sm = sb("row_sm", [P, 7, TPI])
        conv = sb("conv", [128, 2, HW])
        act1 = sb("act1", [128, 2, HW])
        act2 = sb("act2", [128, 2, HW])
        mx1 = sb("mx1", [128, 4])
        mx2 = sb("mx2", [128, 4])
        x1 = sb("x1", [128, 2, HW])
        x1_all = sb("x1_all", [128, N])
        rows = sb("rows", [P, 2, TPI * ROW])
        logits = sb("logits", [P, TILES * E])
        dist = sb("dist", [128, HW])
        junk = conv[:, :, :].rearrange("c q n -> c (q n)").bitcast(mybir.dt.bfloat16).rearrange("c (k n) -> c k n", n=HW)
        exps = sb("exps", [128, HW])
        zsum = sb("zsum", [128, 1])
        bmax = sb("bmax", [128, 2])
        mrow = sb("mrow", [1, 3, 128])
        mcol = sb("mcol", [128, 1])
        prefix = sb("prefix", [128, 1], I32)
        cand = sb("cand", [128, 4], I32)
        cnt = sb("cnt", [128, 4])
        kept = sb("kept", [128, 4])
        tcol = sb("tcol", [128, 4])
        bc = sb("bc", [128, 4, E])
        neg_max = sb("neg_max", [128, E])
        logits_T = sb("logits_T", [P, E * P])
        s_d = sb("s_d", [P, P])
        s_lt = sb("s_lt", [P, P])
        s_eq = sb("s_eq", [P, P])
        s_eqr = sb("s_eqr", [P, P])
        s_lim = sb("s_lim", [P, 1])
        s_tie = sb("s_tie", [P, P])
        s_sel = sb("s_sel", [P, P])
        s_rank = sb("s_rank", [P, P])
        s_edge = sb("s_edge", [P, 2])
        s_abs = sb("s_abs", [P, P + 1], F16)
        s_from = sb("s_from", [P, CAP], F16)
        s_in = sb("s_in", [P, CAP], F16)
        s_cmp = sb("s_cmp", [128, SB, P])
        s_p = sb("s_p", [128, SB])
        gather_idx = sb("gather_idx", [128, 2, SB], U32)
        scatter_idx = sb("scatter_idx", [128, 2, SB], U32)
        w1 = sb("w1", [128, 2, F])
        w2 = sb("w2", [128, 2, FT * C])
        picked = sb("picked", [128, 2, SB, ROW])
        picked_T = sb("picked_T", [128, CAP])
        hid = sb("hid", [128, FT, CAP])
        y_T = sb("y_T", [128, CAP])
        gate_e = sb("gate_e", [128, SB])
        gate = sb("gate", [128, SB])
        y_rows = sb("y_rows", [128, 2, SB, C])
        y_in, o_img = ln_tok, act2

        x_pad_v = x_pad[:, :, :].rearrange("c q (h w) -> c q h w", w=PW)
        tok = psA[0:P, :, :].rearrange("p a (t c) -> p (a t) c", c=C)
        logit_ps = tok[:, TPI, 0:TPI * E].rearrange("p (t e) -> p t e", e=E)

        s_prm, s_w = sem("params_loaded"), sem("weights_loaded")
        s_cz, s_const = sem("const_zeroed"), sem("consts_ready")
        s_setup, s_tiny, s_bnv, s_bns, s_wps, s_wsb = (sem(n) for n in (
            "setup_ready", "setup_math", "bn_var", "bn_std", "weights_turned", "weights_ready"))
        s_xin, s_xres = pair_of("x_in_loaded"), pair_of("x_res_loaded")
        s_t1, s_m1, s_mom1, s_std1, s_sc1, s_n1 = (sem(n) for n in (
            "ln_tokens", "ln_math", "ln_moments", "ln_std", "ln_scale", "ln_normed"))
        s_t2, s_pad, s_conv, s_taken, s_tap, s_h1, s_mx1, s_wm = (sem(n) for n in (
            "ln_channels", "padded", "conv_sums", "conv_taken", "taps_added", "act1_ready", "act1_max", "pw_masked_ready"))
        s_pw, s_h2, s_mx2, s_x1, s_x1c = (sem(n) for n in (
            "pw_sums", "act2_ready", "act2_max", "x1_ready", "x1_kept"))
        s_t3, s_m3, s_mom3, s_std3, s_sc3, s_n3, s_lg, s_rl = (sem(n) for n in (
            "row_tokens", "row_math", "row_moments", "row_std", "row_scale", "row_normed", "logits_ready", "row_logits"))
        s_rows = pair_of("rows_stored")
        s_yz = sem("y_zeroed")
        s_sp, s_sd, s_se, s_cand, s_cnt, s_tot, s_rnd = (sem(n) for n in (
            "search_turned", "search_math", "exps_summed", "candidates", "counted", "totals", "rounds"))
        s_ltt, s_ltc = sem("logits_turned"), sem("logits_T_ready")
        s_tie1, s_pm, s_cex, s_own, s_g, s_idx = (sem(n) for n in (
            "ties_before", "slot_math", "slots_before", "tile_ranks_ready", "slot_ranks", "slots_found"))
        s_gat, s_sca = pair_of("rows_gathered"), pair_of("rows_scattered")
        s_w1, s_w2 = pair_of("w1_loaded"), pair_of("w2_loaded")
        s_pt, s_ptc, s_l1, s_gelu, s_l2, s_yb, s_bt, s_yr = (sem(n) for n in (
            "picked_turned", "picked_T_ready", "hidden_sums", "hidden_ready", "out_sums", "out_biased", "out_turned", "out_rows"))
        s_ge, s_gt, s_si = sem("gate_exp"), sem("gate_ready"), sem("scatter_idx_ready")
        s_yl, s_fo = pair_of("y_loaded"), pair_of("out_stored")
        s_ft, s_fa = sem("final_turned"), sem("final_added")
        s_inv1, s_inv3, s_tapn, s_sdi, s_pd = (sem(n) for n in (
            "ln_inverse", "row_inverse", "inner_taps", "search_inner", "slot_count"))

        s_pool, s_act = sem("pool_past_waits"), sem("act_past_waits")

        block = ctx.enter_context(nc.Block())

        PM = 9

        @block.sync
        def _(sp):
            for n, src in enumerate((bn1_g, bn1_b, bn1_m, bn1_v, bn2_g, bn2_b, bn2_m, bn2_v, dw_b, pw_b)):
                sp.dma_start(prm[:, n:n + 1], src.rearrange("(c a) -> c a", a=1)).then_inc(s_prm, 16)
            sp.dma_start(taps_w[:, :], dw_w.rearrange("c a h w -> c (a h w)")).then_inc(s_prm, 16)
            sp.dma_start(pw_raw[:, :], pw_w.rearrange("o c h w -> o (c h w)")).then_inc(s_w, 16)
            sp.dma_start(wr_raw[:, :], Wr).then_inc(s_w, 16)
            sp.dma_start(b1_raw[:, :], b1.rearrange("e (t f) -> (e t) f", f=128)).then_inc(s_w, 16)
            sp.dma_start(b2_raw[:, :], b2).then_inc(s_w, 16)

            def step(pair, u):
                on, img, q, use = image(pair, u, 0)
                if on:
                    if since(img, 2):
                        sp.wait_ge(s_t1, img - 1)
                    sp.dma_start(x_in[:, q:q + 1, :], x_d[:, ds(img, 1), :]).then_inc(s_xin[q], 16)
                on, img, q, use = image(pair, u, 2)
                if on:
                    if since(img, 2):
                        sp.wait_ge(s_x1, img - 1)
                    sp.dma_start(x_res[:, q:q + 1, :], x_d[:, ds(img, 1), :]).then_inc(s_xres[q], 16)
                    if isinstance(img, int) and img == 0:
                        sp.wait_ge(s_const, 1)
                    sp.dma_start(y_t[:, ds(img, 1), :, :].rearrange("p i t c -> p (i t) c"),
                                 zero_rows[:, :].rearrange("p (t c) -> p t c", c=C)).then_inc(s_yz, 16)
                on, img, q, use = image(pair, u, 4)
                if on:
                    sp.wait_ge(s_n3, img + 1)
                    sp.wait_ge(s_rl, img + 1)
                    sp.dma_start(rows_t[:, ds(img, 1), :, :].rearrange("p i t c -> p (i t) c"),
                                 rows[:, q, :].rearrange("p (t c) -> p t c", c=ROW)).then_inc(s_rows[q], 16)

            steps(sp, step)

            def load_w(e, q):
                sp.dma_start(w1[:, q:q + 1, :], w1_d[:, ds(e, 1), :]).then_inc(s_w1[q], 16)
                sp.dma_start(w2[:, q, :].rearrange("p (t d) -> p t d", d=C),
                             w2_d[:, ds(e, 1), :, :].rearrange("p e t d -> p (e t) d")).then_inc(s_w2[q], 16)

            for q in range(2):
                load_w(q, q)
            with sp.Fori(0, E // 2 - 1) as pair:
                for q in range(2):
                    sp.wait_ge(s_l2, pair * 4 + 2 * q + 2)
                    load_w(pair * 2 + (q + 2), q)

            sp.wait_ge(s_sca[0], 16 * SB * E // 2)
            sp.wait_ge(s_sca[1], 16 * SB * E // 2)

            def load_y(img, q):
                sp.dma_start(y_in[:, q, :].rearrange("p (t c) -> p t c", c=C),
                             y_t[:, ds(img, 1), :, :].rearrange("p i t c -> p (i t) c")).then_inc(s_yl[q], 16)

            for q in range(2):
                load_y(q, q)
            with sp.Fori(0, B // 2 - 1) as pair:
                for q in range(2):
                    sp.wait_ge(s_ft, pair * 2 + q + 1)
                    load_y(pair * 2 + (q + 2), q)
            for q in range(2):
                sp.wait_ge(s_fo[q], 16 * B // 2)
                sp.wait_ge(s_rows[q], 16 * B // 2)

        @block.gpsimd
        def _(pool):
            nc.gpsimd.memset(ident[:, :], 0.0)
            nc.gpsimd.memset(ones[:, :], 1.0)
            nc.gpsimd.memset(avg[:, :], 1.0 / C)
            nc.gpsimd.memset(eps_c[:, :], LN_C_EPS)
            nc.gpsimd.memset(eps_t[:, :], LN_T_EPS)
            nc.gpsimd.memset(cnt[:, :], 0.0)
            nc.gpsimd.memset(prefix[:, :], 0)
            nc.gpsimd.memset(x_pad[:, :, :], 0.0)
            nc.gpsimd.memset(zero_rows[:, :], 0.0).then_inc(s_cz, 1)
            pool.wait_ge(s_cz, 1)
            nc.gpsimd.affine_select(out=ident[:, :], in_=ident[:, :], compare_op=ALU.not_equal, fill=1.0,
                                    base=0, pattern=[[-1, 128]], channel_multiplier=1)
            nc.gpsimd.iota(tile_row[:, :], pattern=[[1, TPI], [TPI, B]], base=0, channel_multiplier=0,
                           allow_small_or_imprecise_dtypes=True)
            nc.gpsimd.iota(part_i[:, 0:1], pattern=[[0, 1]], base=0, channel_multiplier=1)
            nc.gpsimd.iota(mod_i[:, :], pattern=[[-1, 128]], base=128, channel_multiplier=1)
            nc.gpsimd.iota(bit_table[:, :, :], pattern=[[0, ROUNDS], [1, 4]], base=0, channel_multiplier=0)
            nc.gpsimd.iota(slot_row[:, :], pattern=[[1, CAP]], base=0, channel_multiplier=0,
                           allow_small_or_imprecise_dtypes=True)
            nc.gpsimd.iota(slot_col[:, :], pattern=[[128, SB]], base=0, channel_multiplier=1,
                           allow_small_or_imprecise_dtypes=True).then_inc(s_const, 1)

            def step(pair, u):
                on, img, q, use = image(pair, u, 3)
                if on:
                    pool.wait_ge(s_x1, img + 1)
                    nc.gpsimd.tensor_copy(x1_all[:, ds(img * HW, HW)], x1[:, q, :]).then_inc(s_x1c, 1)

            steps(pool, step)

            def gather(e, q, use):
                pool.wait_ge(s_idx, e + 1)
                pool.sem_inc(s_pool, 1)
                for b in range(SB):
                    nc.gpsimd.indirect_dma_start(
                        out=picked[:, q, b, :], out_offset=None, in_=rows_dram,
                        in_offset=bass.IndirectOffsetOnAxis(ap=gather_idx[:, q, b:b + 1], axis=0),
                    ).then_inc(s_gat[q], 16)

            def scatter(e, q, use):
                pool.wait_ge(s_yr, 2 * e + 2)
                pool.wait_ge(s_si, e + 1)
                if q == 1 or since(e, 1):
                    pool.wait_ge(s_sca[1 - q], (use + q) * (16 * SB))
                pool.sem_inc(s_pool, 1)
                for b in range(SB):
                    nc.gpsimd.indirect_dma_start(
                        out=y_dram, out_offset=bass.IndirectOffsetOnAxis(ap=scatter_idx[:, q, b:b + 1], axis=0),
                        in_=y_rows[:, q, b, :], in_offset=None, compute_op=ALU.add,
                    ).then_inc(s_sca[q], 16)

            for q in range(2):
                pool.wait_ge(s_rows[q], 16 * B // 2)
            pool.wait_ge(s_yz, 16 * B)
            for q in range(2):
                gather(q, q, 0)
            def gather_next(e, q):
                pool.wait_ge(s_pt, e * 2 + 2)
                pool.wait_ge(s_ge, e + 1)
                gather(e + 2, q, None)

            for q in range(2):
                gather_next(q, q)
                scatter(q, q, 0)
            with pool.Fori(1, E // 2 - 1) as pair:
                for q in range(2):
                    gather_next(pair * 2 + q, q)
                    scatter(pair * 2 + q, q, pair)
            for q in range(2):
                scatter(E - 2 + q, q, E // 2 - 1)

        @block.scalar
        def _(act):
            act.wait_ge(s_bnv, 1)
            nc.scalar.activation(fold[:, 2:4], fold[:, 0:2], ACT.Sqrt).then_inc(s_bns, 1)
            act.wait_ge(s_wps, 1)
            nc.scalar.activation(pw_T[:, :], psB[:, 0, 0:128], ACT.Copy)
            nc.scalar.activation(b1_T[:, :], psB[:, 0, 128:128 + E * FT], ACT.Copy)
            nc.scalar.activation(b2_T[:, :], psB[:, 0, 256:256 + E], ACT.Copy).then_inc(s_wsb, 1)
            act.wait_ge(s_setup, 1)
            act.wait_ge(s_const, 1)

            def step(pair, u):
                on, img, q, use = image(pair, u, 0)
                if on:
                    act.wait_ge(s_mom1, img + 1)
                    nc.scalar.activation(ln_sm[:, 4, :], ln_sm[:, 3, :], ACT.Sqrt, bias=eps_c[0:P, :],
                                         scale=1.0 / C).then_inc(s_std1, 1)
                on, img, q, use = image(pair, u, 3)
                if on:
                    if since(img, 2):
                        act.wait_ge(s_x1, img - 1)
                    for h in range(2):
                        act.wait_ge(s_pw, img * 2 + h + 1)
                        nc.scalar.activation(act2[:, q, h * HALF:(h + 1) * HALF], psD[:, h, 0:HALF], ACT.Relu,
                                             bias=fold[:, 9:10], scale=fold[:, 5:6]).then_inc(s_h2, 1)
                on, img, q, use = image(pair, u, 0)
                if on:
                    act.wait_ge(s_sc1, img + 1)
                    if since(img, 2):
                        act.wait_ge(s_t2, img - 1)
                    for t in range(TPI):
                        ins = nc.scalar.activation(ln_tok[:, q, t * C:(t + 1) * C], tok[:, t, :], ACT.Identity,
                                                   bias=ln_sm[:, 6, t:t + 1], scale=ln_sm[:, 5, t:t + 1])
                    ins.then_inc(s_n1, 1)
                on, img, q, use = image(pair, u, 2)
                if on:
                    act.wait_ge(s_tap, img + 1)
                    if since(img, 2):
                        act.wait_ge(s_pw, img * 2 - 2)
                    nc.scalar.activation(act1[:, q, :], conv[:, q, :], ACT.Relu,
                                         bias=fold[:, 8:9], scale=fold[:, 4:5]).then_inc(s_h1, 1)
                on, img, q, use = image(pair, u, 4)
                if on:
                    act.wait_ge(s_mom3, img + 1)
                    nc.scalar.activation(row_sm[:, 4, :], row_sm[:, 3, :], ACT.Sqrt, bias=eps_t[0:P, :],
                                         scale=1.0 / C).then_inc(s_std3, 1)
                    act.wait_ge(s_sc3, img + 1)
                    act.wait_ge(s_rl, img + 1)
                    if since(img, 2):
                        act.wait_ge(s_rows[q], use * 16)
                    for t in range(TPI):
                        ins = nc.scalar.activation(rows[:, q, t * ROW:t * ROW + C], tok[:, t, :], ACT.Identity,
                                                   bias=row_sm[:, 6, t:t + 1], scale=row_sm[:, 5, t:t + 1])
                    ins.then_inc(s_n3, 1)
                on, img, q, use = image(pair, u, 0)
                if on:
                    act.wait_ge(s_t2, img + 1)
                    if since(img, 2):
                        act.wait_ge(s_tap, img - 1)
                        act.wait_ge(s_conv, img * 2 - 2)
                    for a, (lo, n) in enumerate(((0, 16), (16, 12))):
                        ins = nc.scalar.activation(x_pad_v[:, q, 1 + lo:1 + lo + n, 1:1 + W],
                                                   psB[:, a, 0:n * W].rearrange("c (h w) -> c h w", w=W), ACT.Copy)
                    ins.then_inc(s_pad, 1)

            steps(act, step)

            act.wait_ge(s_sd, 3)
            nc.scalar.activation(exps[:, :], dist[:, :], ACT.Exp, scale=-1.0, accum_out=zsum[:, :]).then_inc(s_se, 1)
            for a in range(2):
                act.wait_ge(s_ltt, a + 1)
                nc.scalar.activation(logits_T[:, a * 4 * P:(a + 1) * 4 * P], psD[0:P, a, 0:4 * P],
                                     ACT.Copy).then_inc(s_ltc, 1)

            def expert(e, q, use):
                act.wait_ge(s_gat[q], use * (16 * SB) + 16 * SB)
                if since(e, 1):
                    act.wait_ge(s_gt, e)
                act.sem_inc(s_act, 1)
                nc.scalar.activation(gate_e[:, :], picked[:, q, :, ds(C + e, 1)].rearrange("s b a -> s (b a)"),
                                     ACT.Exp, bias=neg_max[:, ds(e, 1)]).then_inc(s_ge, 1)
                for h in range(2):
                    act.wait_ge(s_pt, e * 2 + h + 1)
                    nc.scalar.activation(picked_T[:, h * HS:(h + 1) * HS], psA[:, h, :], ACT.Copy).then_inc(s_ptc, 1)
                for h in range(2):
                    for f in range(FT):
                        act.wait_ge(s_l1, e * (2 * FT) + (h * FT + f + 1))
                        act.sem_inc(s_act, 1)
                        nc.scalar.activation(hid[:, f, h * HS:(h + 1) * HS], psB[:, f % 2, :], ACT.Gelu,
                                             bias=b1_T[:, ds(e * FT + f, 1)]).then_inc(s_gelu, 1)

            act.wait_ge(s_sd, 9)
            for q in range(2):
                expert(q, q, 0)
            with act.Fori(1, E // 2) as pair:
                for q in range(2):
                    expert(pair * 2 + q, q, pair)

            with act.Fori(0, B // 2) as pair:
                for q in range(2):
                    act.wait_ge(s_fa, pair * 2 + q + 1)
                    act.dma_start(out_d[:, ds(pair * 2 + q, 1), :], o_img[:, q:q + 1, :]).then_inc(s_fo[q], 16)

        @block.tensor
        def _(pe):
            pe.wait_ge(s_const, 1)
            pe.wait_ge(s_w, 64)
            nc.tensor.transpose(psB[:, 0, 0:128], pw_raw[:, :], ident[:, :])
            nc.tensor.transpose(psB[:, 0, 128:128 + E * FT], b1_raw[:, :], ident[0:E * FT, 0:E * FT])
            nc.tensor.transpose(psB[:, 0, 256:256 + E], b2_raw[:, :], ident[0:E, 0:E])
            nc.tensor.matmul(psB[:, 0, 384:384 + E], avg[:, :], wr_raw[:, :], start=True, stop=True).then_inc(s_wps, 1)
            pe.wait_ge(s_setup, 1)
            pe.wait_ge(s_wsb, 1)

            def conv_half(img, q, h):
                for n in range(PE_TAPS):
                    dy, dx = TAPS[n]
                    y0 = h * LINES + dy
                    ins = nc.tensor.matmul(psC[:, h, 0:HALF].rearrange("c (h w) -> c h w", w=W), tap_diag[:, n, :],
                                           x_pad_v[:, q, y0:y0 + LINES, dx:dx + W],
                                           start=(n == 0), stop=(n == PE_TAPS - 1))
                ins.then_inc(s_conv, 1)

            def step(pair, u):
                on, img, q, use = image(pair, u, 0)
                if on:
                    pe.wait_ge(s_xin[q], use * 16 + 16)
                    on4, img4, _, _ = image(pair, u, 5)
                    if on4:
                        pe.wait_ge(s_n3, img4 + 1)
                        pe.wait_ge(s_lg, img4 + 1)
                    for t in range(TPI):
                        ins = nc.tensor.transpose(tok[:, t, :], x_in[:, q, t * P:(t + 1) * P], ident[:, :])
                    ins.then_inc(s_t1, 1)
                on, img, q, use = image(pair, u, 3)
                if on:
                    pe.wait_ge(s_wm, img + 1)
                    if since(img, 1):
                        pe.wait_ge(s_h2, img * 2)
                    for h in range(2):
                        nc.tensor.matmul(psD[:, h, 0:HALF], pw_masked[:, q, :], act1[:, q, h * HALF:(h + 1) * HALF],
                                         start=True, stop=True).then_inc(s_pw, 1)
                on1, img1, q1, use1 = image(pair, u, 1)
                if on1:
                    pe.wait_ge(s_pad, img1 + 1)
                    if since(img1, 1):
                        pe.wait_ge(s_taken, img1)
                    conv_half(img1, q1, 0)
                on, img, q, use = image(pair, u, 4)
                if on:
                    on0, img0, _, _ = image(pair, u, 0)
                    if on0:
                        pe.wait_ge(s_n1, img0 + 1)
                    elif since(img, 1):
                        pe.wait_ge(s_n3, img)
                        pe.wait_ge(s_lg, img)
                    pe.wait_ge(s_x1, img + 1)
                    for t in range(TPI):
                        nc.tensor.transpose(tok[:, t, :], x1[:, q, t * P:(t + 1) * P], ident[:, :])
                    for t in range(TPI):
                        ins = nc.tensor.matmul(logit_ps[:, t, :], x1[:, q, t * P:(t + 1) * P], wr_c[:, :],
                                               start=True, stop=True)
                    ins.then_inc(s_t3, 1)
                if on1:
                    conv_half(img1, q1, 1)
                on, img, q, use = image(pair, u, 0)
                if on:
                    pe.wait_ge(s_n1, img + 1)
                    if since(img, 1):
                        pe.wait_ge(s_pad, img)
                    for t in range(TPI):
                        ins = nc.tensor.transpose(psB[:, t // 4, (t % 4) * P:(t % 4 + 1) * P],
                                                  ln_tok[:, q, t * C:(t + 1) * C], ident[0:P, 0:P])
                    ins.then_inc(s_t2, 1)

            steps(pe, step)

            pe.wait_ge(s_n3, B)
            pe.wait_ge(s_lg, B)
            by_tile = logits[:, :].rearrange("p (t k) -> p t k", t=TPI)
            for t in range(TPI):
                ins = nc.tensor.transpose(psA[:, t // 4, (t % 4) * P:(t % 4 + 1) * P], by_tile[:, t, :], ident[0:P, 0:P])
            ins.then_inc(s_sp, 1)
            pe.wait_ge(s_sd, 1)
            nc.tensor.transpose(psB[0:1, 0, 0:128], bmax[:, 0:1], ident[:, :]).then_inc(s_sp, 1)
            pe.wait_ge(s_sd, 2)
            nc.tensor.transpose(psB[:, 0, 128:129], mrow[:, 2, :], ident[0:1, 0:1]).then_inc(s_sp, 1)
            pe.wait_ge(s_h2, 2 * B)
            by_expert = logits[:, :].rearrange("p (k e) -> p e k", e=E)
            for a in range(2):
                for e in range(4 * a, 4 * a + 4):
                    ins = nc.tensor.transpose(psD[0:P, a, (e % 4) * P:(e % 4 + 1) * P], by_expert[:, e, :], ident[0:P, 0:P])
                ins.then_inc(s_ltt, 1)
            pe.wait_ge(s_se, 1)
            nc.tensor.matmul(psB[:, 1, 0:1], same_expert[:, :], zsum[:, :], start=True, stop=True).then_inc(s_sp, 1)
            with pe.Fori(0, ROUNDS + 1) as r:
                pe.wait_ge(s_cnt, r + 1)
                nc.tensor.matmul(psC[:, 0, 0:4], same_expert[:, :], cnt[:, :], start=True, stop=True).then_inc(s_tot, 1)
            pe.wait_ge(s_sd, 7)
            for n in range(4):
                ins = nc.tensor.transpose(psB[:, 0, n * 128:(n + 1) * 128], tcol[:, n:n + 1].to_broadcast([128, 128]), ident[:, :])
            ins.then_inc(s_sp, 1)

            def ties(e):
                pe.wait_ge(s_pm, e * PM + 3)
                nc.tensor.matmul(psD[0:P, 0, 120:121], before[:, :], s_eqr[:, P - 1:P], start=True, stop=True).then_inc(s_tie1, 1)

            def slots_before(e):
                pe.wait_ge(s_pm, e * PM + 7)
                nc.tensor.matmul(psD[0:P, 0, 121:122], before[:, :], s_rank[:, P - 1:P], start=True, stop=True).then_inc(s_cex, 1)

            def slot_ranks(e):
                pe.wait_ge(s_own, e + 1)
                for b in range(SB):
                    ins = nc.tensor.matmul(psD[:, b // 4, (b % 4) * 128:(b % 4) * 128 + P + 1], s_in[:, b * 128:(b + 1) * 128],
                                           s_abs[:, :], start=True, stop=True)
                ins.then_inc(s_g, 1)

            pe.wait_ge(s_ltc, 2)
            for e in range(2):
                if e:
                    pe.wait_ge(s_idx, e)
                ties(e)
                slots_before(e)
                slot_ranks(e)

            def hidden(e, q, h):
                for f in range(FT):
                    n = h * FT + f
                    if n >= 2 or since(e, 1):
                        pe.wait_ge(s_gelu, e * (2 * FT) + n - 1)
                    nc.tensor.matmul(psB[:, f % 2, :], w1[:, q, f * 128:(f + 1) * 128], picked_T[:, h * HS:(h + 1) * HS],
                                     start=True, stop=True).then_inc(s_l1, 1)

            def down(e, q, h):
                pe.wait_ge(s_gelu, e * (2 * FT) + (h + 1) * FT)
                if since(e, 1):
                    pe.wait_ge(s_yb, e * 2 + h - 1)
                for f in range(FT):
                    ins = nc.tensor.matmul(psC[:, h, :], w2[:, q, f * C:(f + 1) * C], hid[:, f, h * HS:(h + 1) * HS],
                                           start=(f == 0), stop=(f == FT - 1))
                ins.then_inc(s_l2, 1)

            def back(e, h):
                pe.wait_ge(s_yb, e * 2 + h + 1)
                for b in range(4):
                    ins = nc.tensor.transpose(psA[:, h, b * 128:(b + 1) * 128], y_T[:, h * HS + b * 128:h * HS + (b + 1) * 128], ident[:, :])
                ins.then_inc(s_bt, 1)

            def expert(e, q, use, ahead):
                pe.wait_ge(s_gat[q], use * (16 * SB) + 16 * SB)
                if since(e, 1):
                    pe.wait_ge(s_yr, e * 2)
                for h in range(2):
                    for b in range(4):
                        ins = nc.tensor.transpose(psA[:, h, b * 128:(b + 1) * 128], picked[:, q, h * 4 + b, 0:C], ident[:, :])
                    ins.then_inc(s_pt, 1)
                pe.wait_ge(s_w1[q], use * 16 + 16)
                pe.wait_ge(s_ptc, e * 2 + 1)
                hidden(e, q, 0)
                if ahead:
                    pe.wait_ge(s_idx, e + 2)
                    ties(e + 2)
                pe.wait_ge(s_ptc, e * 2 + 2)
                hidden(e, q, 1)
                if ahead:
                    slots_before(e + 2)
                pe.wait_ge(s_w2[q], use * 16 + 16)
                down(e, q, 0)
                down(e, q, 1)
                back(e, 0)
                if ahead:
                    slot_ranks(e + 2)
                back(e, 1)

            for q in range(2):
                expert(q, q, 0, True)
            with pe.Fori(1, E // 2 - 1) as pair:
                for q in range(2):
                    expert(pair * 2 + q, q, pair, True)
            for q in range(2):
                expert(E - 2 + q, q, E // 2 - 1, False)

            regions = (psB, psD)
            pe.wait_ge(s_gelu, E * 2 * FT)
            pe.wait_ge(s_idx, E)

            def turn_back(img, q, use):
                pe.wait_ge(s_yl[q], use * 16 + 16)
                if since(img, 2):
                    pe.wait_ge(s_fa, img - 1)
                for t in range(TPI):
                    ins = nc.tensor.transpose(regions[q][:, t // 4, (t % 4) * P:(t % 4 + 1) * P],
                                              y_in[:, q, t * C:(t + 1) * C], ident[0:P, 0:P])
                ins.then_inc(s_ft, 1)

            for q in range(2):
                turn_back(q, q, 0)
            with pe.Fori(1, B // 2) as pair:
                for q in range(2):
                    turn_back(pair * 2 + q, q, pair)

        @block.vector
        def _(dve):
            dve.wait_ge(s_prm, 16 * 11)
            pv = prm[:, 0:8].rearrange("c (n k) -> c k n", k=4)
            nc.vector.tensor_scalar(fold[:, 0:2], pv[:, 3, :], BN_EPS, None, ALU.add).then_inc(s_bnv, 1)
            nc.vector.tensor_tensor(fold[:, 6:8], prm[:, 8:10], pv[:, 2, :], ALU.subtract).then_inc(s_tiny, 1)
            dve.wait_ge(s_bns, 1)
            nc.vector.reciprocal(fold[:, 10:12], fold[:, 2:4]).then_inc(s_tiny, 1)
            dve.wait_ge(s_tiny, 2)
            nc.vector.tensor_tensor(fold[:, 4:6], fold[:, 10:12], pv[:, 0, :], ALU.mult).then_inc(s_tiny, 1)
            dve.wait_ge(s_tiny, 3)
            nc.vector.tensor_tensor(fold[:, 8:10], fold[:, 6:8], fold[:, 4:6], ALU.mult).then_inc(s_tiny, 1)
            dve.wait_ge(s_tiny, 4)
            nc.vector.tensor_tensor(fold[:, 8:10], fold[:, 8:10], pv[:, 1, :], ALU.add)
            dve.wait_ge(s_const, 1)
            for n in range(PE_TAPS):
                nc.vector.tensor_scalar(tap_diag[:, n, :], ident[:, :], taps_w[:, n:n + 1], None, ALU.mult)
            nc.vector.tensor_scalar(mod_i[:, :], mod_i[:, :], E - 1, None, ALU.bitwise_and).then_inc(s_tiny, 1)
            nc.vector.tensor_scalar(bit_table[:, ROUNDS - 1, :], bit_table[:, ROUNDS - 1, :], 1, None, ALU.min)
            for r in range(ROUNDS - 1):
                nc.vector.tensor_scalar(bit_table[:, r, :], bit_table[:, r, :], SHIFTS[r], None, ALU.logical_shift_left)
            nc.vector.tensor_scalar(part_i[:, 1:2], part_i[:, 0:1], B - 1, None, ALU.bitwise_and)
            nc.vector.tensor_scalar(part_i[:, 2:3], part_i[:, 0:1], 4, None, ALU.logical_shift_right).then_inc(s_tiny, 1)
            dve.wait_ge(s_tiny, 6)
            nc.vector.scalar_tensor_tensor(tile_col[:, :], part_i[:, 1:2], float(TPI), part_i[:, 2:3], ALU.mult, ALU.add)\
                .then_inc(s_tiny, 1)
            dve.wait_ge(s_tiny, 7)
            nc.vector.tensor_scalar(before[:, :], tile_row[:, :], tile_col[:, :], None, ALU.is_gt)
            nc.vector.tensor_copy(s_abs[:, P:P + 1], tile_col[:, :])
            nc.vector.tensor_scalar(same_expert[:, :], mod_i[:, :], 0, None, ALU.is_equal)
            dve.wait_ge(s_wps, 1)
            dve.wait_ge(s_wsb, 1)
            nc.vector.tensor_tensor(wr_c[:, :], wr_raw[:, :], psB[:, 0, 384:384 + E], ALU.subtract).then_inc(s_setup, 1)

            def moments(st, sm, s_math, s_mom, img):
                for t in range(TPI):
                    ins = nc.vector.bn_stats(st[:, t, :], tok[:, t, :])
                ins.then_inc(s_math, 1)
                dve.wait_ge(s_math, img * 3 + 1)
                nc.vector.tensor_tensor(sm[:, 1, :], st[:, :, 1], st[:, :, 4], ALU.subtract)
                nc.vector.tensor_tensor(sm[:, 2, :], st[:, :, 2], st[:, :, 5], ALU.add)
                nc.vector.tensor_tensor(sm[:, 0, :], st[:, :, 1], st[:, :, 4], ALU.add).then_inc(s_math, 1)
                dve.wait_ge(s_math, img * 3 + 2)
                nc.vector.scalar_tensor_tensor(sm[:, 1, :], sm[:, 1, :], C / 4.0, sm[:, 1, :], ALU.mult, ALU.mult)\
                    .then_inc(s_math, 1)
                dve.wait_ge(s_math, img * 3 + 3)
                nc.vector.tensor_tensor(sm[:, 3, :], sm[:, 1, :], sm[:, 2, :], ALU.add).then_inc(s_mom, 1)

            def scales(sm, s_std, s_sc, img):
                dve.wait_ge(s_std, img + 1)
                nc.vector.reciprocal(sm[:, 5, :], sm[:, 4, :]).then_inc(s_sc[0], 1)
                dve.wait_ge(s_sc[0], img + 1)
                nc.vector.scalar_tensor_tensor(sm[:, 6, :], sm[:, 0, :], -0.5, sm[:, 5, :], ALU.mult, ALU.mult)\
                    .then_inc(s_sc[1], 1)

            def tap(q, n, h, first):
                dy, dx = TAPS[PE_TAPS + n]
                y0, lines = (h * LINES, LINES) if first else (0, H)
                o = conv[:, q, y0 * W:(y0 + lines) * W].rearrange("c (h w) -> c h w", w=W)
                acc = psC[:, h, 0:HALF].rearrange("c (h w) -> c h w", w=W) if first else o
                return nc.vector.scalar_tensor_tensor(o, x_pad_v[:, q, y0 + dy:y0 + dy + lines, dx:dx + W],
                                                      taps_w[:, PE_TAPS + n:PE_TAPS + n + 1], acc, ALU.mult, ALU.add)

            def step(pair, u):
                on2, img2, q2, _ = image(pair, u, 2)
                if on2:
                    dve.wait_ge(s_conv, img2 * 2 + 2)
                    if since(img2, 2):
                        dve.wait_ge(s_h1, img2 - 1)
                    tap(q2, 0, 0, True)
                    tap(q2, 0, 1, True).then_inc(s_taken, 1)
                on0, img0, q0, _ = image(pair, u, 0)
                if on0:
                    dve.wait_ge(s_t1, img0 + 1)
                    moments(ln_st, ln_sm, s_m1, s_mom1, img0)
                if on2:
                    for n in range(1, DVE_TAPS):
                        if n == 1:
                            dve.wait_ge(s_taken, img2 + 1)
                        else:
                            dve.wait_ge(s_tapn, img2 * (DVE_TAPS - 2) + n - 1)
                        ins = tap(q2, n, 0, False)
                        ins.then_inc(s_tapn if n < DVE_TAPS - 1 else s_tap, 1)
                if on0:
                    scales(ln_sm, s_std1, (s_inv1, s_sc1), img0)
                on, img, q, use = image(pair, u, 3)
                if on:
                    dve.wait_ge(s_h2, img * 2 + 2)
                    nc.vector.reduce_max(mx2[:, 0:1], act2[:, q, :], AX_X).then_inc(s_mx2, 1)
                    dve.wait_ge(s_mx2, img * 2 + 1)
                    nc.vector.tensor_scalar(mx2[:, 1:2], mx2[:, 0:1], PW_THRESH, None, ALU.is_ge).then_inc(s_mx2, 1)
                    dve.wait_ge(s_mx2, img * 2 + 2)
                    dve.wait_ge(s_xres[q], use * 16 + 16)
                    if since(img, 2):
                        dve.wait_ge(s_t3, img - 1)
                        dve.wait_ge(s_x1c, img - 1)
                    nc.vector.scalar_tensor_tensor(x1[:, q, :], act2[:, q, :], mx2[:, 1:2], x_res[:, q, :],
                                                   ALU.mult, ALU.add).then_inc(s_x1, 1)
                on4, img4, q4, use4 = image(pair, u, 4)
                if on4:
                    dve.wait_ge(s_t3, img4 + 1)
                    moments(row_st, row_sm, s_m3, s_mom3, img4)
                if on2:
                    dve.wait_ge(s_h1, img2 + 1)
                    nc.vector.reduce_max(mx1[:, 0:1], act1[:, q2, :], AX_X).then_inc(s_mx1, 1)
                    dve.wait_ge(s_mx1, img2 * 2 + 1)
                    nc.vector.tensor_scalar(mx1[:, 1:2], mx1[:, 0:1], DW_THRESH, None, ALU.is_ge).then_inc(s_mx1, 1)
                    dve.wait_ge(s_mx1, img2 * 2 + 2)
                    if since(img2, 2):
                        dve.wait_ge(s_pw, img2 * 2 - 2)
                    if isinstance(img2, int) and img2 == 0:
                        dve.wait_ge(s_wsb, 1)
                    nc.vector.tensor_scalar(pw_masked[:, q2, :], pw_T[:, :], mx1[:, 1:2], None, ALU.mult).then_inc(s_wm, 1)
                if on4:
                    scales(row_sm, s_std3, (s_inv3, s_sc3), img4)
                    inv = row_sm[:, 5, :].unsqueeze(2).to_broadcast([P, TPI, E])
                    lg = logits[:, :].rearrange("p (t k) -> p t k", t=TPI)[:, :, ds(img4 * E, E)]
                    nc.vector.tensor_tensor(lg, logit_ps, inv, ALU.mult).then_inc(s_lg, 1)
                    if since(img4, 2):
                        dve.wait_ge(s_rows[q4], use4 * 16)
                    nc.vector.tensor_tensor(rows[:, q4, :].rearrange("p (t c) -> p t c", c=ROW)[:, :, C:ROW], logit_ps, inv,
                                            ALU.mult).then_inc(s_rl, 1)

            steps(dve, step)

            la = psA[:, 0, 0:4 * P]
            lb = psA[:, 1, 0:3 * P]
            dve.wait_ge(s_sp, 1)
            nc.vector.reduce_max(bmax[:, 0:1], la, AX_X)
            nc.vector.reduce_max(bmax[:, 1:2], lb, AX_X).then_inc(s_sdi, 1)
            dve.wait_ge(s_sdi, 1)
            nc.vector.tensor_tensor(bmax[:, 0:1], bmax[:, 0:1], bmax[:, 1:2], ALU.max).then_inc(s_sd, 1)
            dve.wait_ge(s_sp, 2)
            nc.vector.tensor_reduce(mrow[:, 1, 0:E], psB[0:1, 0, 0:128].rearrange("a (i e) -> a e i", e=E), AX_X, ALU.max)\
                .then_inc(s_sdi, 1)
            dve.wait_ge(s_sdi, 2)
            nc.vector.tensor_copy(mrow[:, 2, :].rearrange("a (i e) -> a i e", e=E),
                                  mrow[:, 1, 0:E].unsqueeze(1).to_broadcast([1, B, E])).then_inc(s_sd, 1)
            dve.wait_ge(s_sp, 3)
            nc.vector.tensor_copy(mcol[:, :], psB[:, 0, 128:129]).then_inc(s_sdi, 1)
            dve.wait_ge(s_sdi, 3)
            nc.vector.tensor_scalar(dist[:, 0:4 * P], la, mcol[:, :], -1.0, ALU.subtract, ALU.mult)
            nc.vector.tensor_scalar(dist[:, 4 * P:HW], lb, mcol[:, :], -1.0, ALU.subtract, ALU.mult).then_inc(s_sd, 1)
            dve.wait_ge(s_sd, 3)
            with dve.Fori(0, ROUNDS) as r:
                nc.vector.tensor_scalar(cand[:, :], bit_table[:, ds(r, 1), :].rearrange("p a b -> p (a b)"), prefix[:, :], None,
                                        ALU.bitwise_or).then_inc(s_cand, 1)
                dve.wait_ge(s_cand, r * 3 + 1)
                for n in range(1, 4):
                    ins = nc.vector.tensor_scalar(junk[:, n, :], dist[:, :], cand[:, n:n + 1].bitcast(F32), None, ALU.is_lt, ALU.add,
                                                  accum_out=cnt[:, n:n + 1])
                ins.then_inc(s_cnt, 1)
                dve.wait_ge(s_tot, r + 1)
                nc.vector.scalar_tensor_tensor(kept[:, :], psC[:, 0, 0:4], float(CAP), cand[:, :].bitcast(F32),
                                               ALU.is_lt, ALU.mult).then_inc(s_cand, 1)
                dve.wait_ge(s_cand, r * 3 + 2)
                nc.vector.reduce_max(prefix[:, :].bitcast(F32), kept[:, :], AX_X).then_inc(s_cand, 1)
                dve.wait_ge(s_cand, r * 3 + 3)
            nc.vector.tensor_scalar(junk[:, 0, :], dist[:, :], prefix[:, :].bitcast(F32), None, ALU.is_lt, ALU.add,
                                    accum_out=cnt[:, 1:2]).then_inc(s_cnt, 1)
            nc.vector.tensor_copy(tcol[:, 0:1], prefix[:, :].bitcast(F32)).then_inc(s_sd, 1)
            nc.vector.tensor_copy(tcol[:, 2:3], mcol[:, :]).then_inc(s_sd, 1)
            dve.wait_ge(s_sp, 4)
            nc.vector.reciprocal(tcol[:, 3:4], psB[:, 1, 0:1]).then_inc(s_sd, 1)
            dve.wait_ge(s_tot, ROUNDS + 1)
            nc.vector.tensor_scalar(tcol[:, 1:2], psC[:, 0, 1:2], -1.0, float(CAP), ALU.mult, ALU.add).then_inc(s_sd, 1)
            dve.wait_ge(s_sp, 5)
            nc.vector.tensor_copy(bc[:, :, :], psB[:, 0, :].rearrange("p (n k) -> p n k", n=4)[:, :, 0:E]).then_inc(s_sd, 1)
            dve.wait_ge(s_sd, 8)
            nc.vector.tensor_scalar(neg_max[:, :], bc[:, 2, :], -1.0, None, ALU.mult).then_inc(s_sd, 1)
            dve.wait_ge(s_ltc, 2)

            def col(n, e):
                return bc[0:P, n, ds(e, 1)]

            def slots_a(e):
                nc.vector.tensor_scalar(s_d[:, :], logits_T[:, ds(e * P, P)], col(2, e), -1.0, ALU.subtract, ALU.mult)\
                    .then_inc(s_pm, 1)
                dve.wait_ge(s_pm, e * PM + 1)
                nc.vector.tensor_scalar(s_eq[:, :], s_d[:, :], col(0, e), None, ALU.is_equal).then_inc(s_pm, 1)
                nc.vector.tensor_scalar(s_lt[:, :], s_d[:, :], col(0, e), None, ALU.is_lt)
                dve.wait_ge(s_pm, e * PM + 2)
                nc.vector.tensor_tensor_scan(s_eqr[:, :], ones[0:P, 0:P], s_eq[:, :], 0.0, ALU.mult, ALU.add).then_inc(s_pm, 1)

            def slots_b(e):
                dve.wait_ge(s_tie1, e + 1)
                nc.vector.tensor_tensor(s_lim[:, :], col(1, e), psD[0:P, 0, 120:121], ALU.subtract).then_inc(s_pm, 1)
                dve.wait_ge(s_pm, e * PM + 4)
                nc.vector.scalar_tensor_tensor(s_tie[:, :], s_eqr[:, :], s_lim[:, :], s_eq[:, :], ALU.is_le, ALU.mult)\
                    .then_inc(s_pm, 1)
                dve.wait_ge(s_pm, e * PM + 5)
                nc.vector.tensor_tensor(s_sel[:, :], s_tie[:, :], s_lt[:, :], ALU.add).then_inc(s_pm, 1)
                dve.wait_ge(s_pm, e * PM + 6)
                nc.vector.tensor_tensor_scan(s_rank[:, :], ones[0:P, 0:P], s_sel[:, :], 0.0, ALU.mult, ALU.add).then_inc(s_pm, 1)

            def slots_c(e):
                dve.wait_ge(s_cex, e + 1)
                nc.vector.tensor_copy(s_edge[:, 0:1], psD[0:P, 0, 121:122])
                nc.vector.tensor_tensor(s_edge[:, 1:2], s_rank[:, P - 1:P], psD[0:P, 0, 121:122], ALU.add).then_inc(s_pm, 1)
                dve.wait_ge(s_pm, e * PM + 8)
                nc.vector.tensor_scalar(s_abs[:, 0:P], s_rank[:, :], s_edge[:, 0:1], None, ALU.add)
                nc.vector.tensor_scalar(s_from[:, :], slot_row[:, :], s_edge[:, 0:1], None, ALU.is_ge).then_inc(s_pm, 1)
                dve.wait_ge(s_pm, e * PM + 9)
                nc.vector.scalar_tensor_tensor(s_in[:, :], slot_row[:, :], s_edge[:, 1:2], s_from[:, :], ALU.is_lt, ALU.mult)\
                    .then_inc(s_own, 1)

            def slots_d(e, q, last_use):
                dve.wait_ge(s_g, e + 1)
                ranks = psD[:, :, :].rearrange("p a (b k) -> p (a b) k", k=128)
                nc.vector.tensor_tensor(s_cmp[:, :, :], ranks[:, :, 0:P], slot_col[:, :].unsqueeze(2).to_broadcast([128, SB, P]),
                                        ALU.is_le).then_inc(s_pd, 1)
                dve.wait_ge(s_pd, e * 2 + 1)
                nc.vector.reduce_sum(s_p[:, :], s_cmp[:, :, :], AX_X).then_inc(s_pd, 1)
                dve.wait_ge(s_pd, e * 2 + 2)
                if last_use is not None:
                    dve.wait_ge(s_gat[q], last_use * (16 * SB))
                nc.vector.scalar_tensor_tensor(gather_idx[:, q, :], ranks[:, :, P], float(P), s_p[:, :], ALU.mult, ALU.add)\
                    .then_inc(s_idx, 1)

            for e in range(2):
                slots_a(e)
                slots_b(e)
                slots_c(e)
                slots_d(e, e, None)

            def bias_out(e, h):
                dve.wait_ge(s_l2, e * 2 + h + 1)
                if since(e, 1):
                    dve.wait_ge(s_bt, e * 2 - 1 + h)
                nc.vector.tensor_scalar(y_T[:, h * HS:(h + 1) * HS], psC[:, h, :], b2_T[:, ds(e, 1)], None, ALU.add)\
                    .then_inc(s_yb, 1)

            def weigh(e, q, use, h):
                dve.wait_ge(s_bt, e * 2 + h + 1)
                if since(e, 2):
                    dve.wait_ge(s_sca[q], use * (16 * SB))
                nc.vector.tensor_tensor(y_rows[:, q, 4 * h:4 * h + 4, :], psA[:, h, :].rearrange("s (b d) -> s b d", d=C),
                                        gate[:, 4 * h:4 * h + 4].unsqueeze(2).to_broadcast([128, 4, C]), ALU.mult).then_inc(s_yr, 1)

            def expert(e, q, use, ahead):
                if since(e, 2):
                    dve.wait_ge(s_sca[q], use * (16 * SB))
                nc.vector.tensor_copy(scatter_idx[:, q, :], gather_idx[:, q, :]).then_inc(s_si, 1)
                dve.wait_ge(s_ge, e + 1)
                if since(e, 1):
                    dve.wait_ge(s_yr, e * 2)
                nc.vector.tensor_scalar(gate[:, :], gate_e[:, :], bc[:, 3, ds(e, 1)], None, ALU.mult).then_inc(s_gt, 1)
                if ahead:
                    slots_a(e + 2)
                    slots_b(e + 2)
                    slots_c(e + 2)
                bias_out(e, 0)
                bias_out(e, 1)
                dve.wait_ge(s_gt, e + 1)
                weigh(e, q, use, 0)
                if ahead:
                    dve.wait_ge(s_si, e + 1)
                    slots_d(e + 2, q, use + 1)
                weigh(e, q, use, 1)

            for q in range(2):
                expert(q, q, 0, True)
            with dve.Fori(1, E // 2 - 1) as pair:
                for q in range(2):
                    expert(pair * 2 + q, q, pair, True)
            for q in range(2):
                expert(E - 2 + q, q, E // 2 - 1, False)

            regions = (psB, psD)

            dve.wait_ge(s_x1c, B)

            def add_up(img, q, use):
                dve.wait_ge(s_ft, img + 1)
                if since(img, 2):
                    dve.wait_ge(s_fo[q], use * 16)
                nc.vector.tensor_tensor(o_img[:, q, 0:4 * P], regions[q][:, 0, 0:4 * P], x1_all[:, ds(img * HW, 4 * P)], ALU.add)
                nc.vector.tensor_tensor(o_img[:, q, 4 * P:HW], regions[q][:, 1, 0:3 * P],
                                        x1_all[:, ds(img * HW + 4 * P, 3 * P)], ALU.add).then_inc(s_fa, 1)

            for q in range(2):
                add_up(q, q, 0)
            with dve.Fori(1, B // 2) as pair:
                for q in range(2):
                    add_up(pair * 2 + q, q, pair)


_INS = ['x', 'L0_conv_dw_w', 'L0_conv_dw_b', 'L0_conv_bn1_g', 'L0_conv_bn1_b', 'L0_conv_bn1_m', 'L0_conv_bn1_v',
        'L0_conv_pw_w', 'L0_conv_pw_b', 'L0_conv_bn2_g', 'L0_conv_bn2_b', 'L0_conv_bn2_m', 'L0_conv_bn2_v',
        'L0_ffn_Wr', 'L0_ffn_W1', 'L0_ffn_b1', 'L0_ffn_W2', 'L0_ffn_b2']
_OUTS = [((B, C, H, W), 'float32')]


def kernel(**inputs):
    import numpy as _np
    import concourse.bacc as _bacc
    from concourse import mybir as _mybir
    from concourse.bass_utils import run_bass_kernel_spmd as _run

    nc = _bacc.Bacc("TRN2", target_bir_lowering=False, num_devices=1)
    arrays, args = {}, []
    for name in _INS:
        a = _np.ascontiguousarray(inputs[name])
        arrays[f"in_{name}_dram"] = a
        args.append(nc.dram_tensor(f"in_{name}_dram", a.shape, _mybir.dt.from_np(a.dtype), kind="ExternalInput").ap())
    for i, (shape, dtype) in enumerate(_OUTS):
        dt = _mybir.dt.from_np(_np.dtype(dtype))
        args.append(nc.dram_tensor(f"out_{i}_dram", shape, dt, kind="ExternalOutput").ap())
    build(nc, *args)
    r = _run(nc, [arrays], core_ids=[0])
    got = tuple(r.results[0][f"out_{i}_dram"] for i in range(len(_OUTS)))
    return got[0]
```

```python
from contextlib import ExitStack

import concourse.bass as bass
from concourse import mybir

ALU = mybir.AluOpType
ACT = mybir.ActivationFunctionType
AX_X = mybir.AxisListType.X
F32 = mybir.dt.float32
F16 = mybir.dt.float16
I32 = mybir.dt.int32
U32 = mybir.dt.uint32
ds = bass.ds

B, C, H, W = 16, 128, 28, 28
HW = H * W
P = 112
TPI = HW // P
TILES = B * TPI
N = B * HW
E, F, CAP = 8, 512, 1024
SB = CAP // 128
FT = F // 128
ROW = C + E
HALF = HW // 2
LINES = H // 2
PW = W + 2
HS = CAP // 2
DW_THRESH, PW_THRESH = 4.0, 0.001
BN_EPS, LN_C_EPS, LN_T_EPS = 1e-5, 1e-6, 1e-5

PE_TAPS = 5
TAPS = [(dy, dx) for dy in range(3) for dx in range(3)]
DVE_TAPS = len(TAPS) - PE_TAPS

LOOP_FIRST, LOOP_END, LAST_PAIR = 3, B // 2 - 1, B // 2 + 3
SHIFTS = list(range(29, 0, -2)) + [0]
ROUNDS = len(SHIFTS)
OFFSET = HW / 2
LIMIT = float(CAP - B * OFFSET)
UNROLL = 5


def steps(eng, step):
    for pair in range(LOOP_FIRST):
        for u in range(2):
            step(pair, u)
    with eng.Fori(LOOP_FIRST, LOOP_END) as pair:
        for u in range(2):
            step(pair, u)
    for pair in range(LOOP_END, LAST_PAIR):
        for u in range(2):
            step(pair, u)


def image(pair, u, lag):
    o = u - lag
    img, use = pair * 2 + o, pair + o // 2
    active = not isinstance(pair, int) or 0 <= img < B
    return active, img, o % 2, use


def since(number, first):
    return not isinstance(number, int) or number >= first


def build(nc, x, dw_w, dw_b, bn1_g, bn1_b, bn1_m, bn1_v, pw_w, pw_b, bn2_g, bn2_b, bn2_m, bn2_v,
          Wr, W1, b1, W2, b2, out):
    x_d = x.rearrange("b c h w -> c b (h w)")
    out_d = out.rearrange("b c h w -> c b (h w)")
    w1_d = W1.rearrange("e d f -> d e f")
    w2_d = W2.rearrange("e (t p) d -> p e t d", p=128)

    with ExitStack() as ctx:
        def sb(name, shape, dt=F32):
            return ctx.enter_context(nc.sbuf_tensor(name, shape, dt))

        def sem(name):
            return ctx.enter_context(nc.semaphore(name))

        def pair_of(name):
            return [sem(f"{name}{q}") for q in range(2)]

        rows_dram = nc.dram_tensor("token_rows", (N, ROW), F32).ap()
        y_dram = nc.dram_tensor("moe_sum", (N, C), F32).ap()
        rows_t = rows_dram.rearrange("(i t p) c -> p i t c", p=P, t=TPI)
        y_t = y_dram.rearrange("(i t p) c -> p i t c", p=P, t=TPI)

        psA, psB, psC, psD = (ctx.enter_context(nc.psum_tensor(f"ps{n}", [128, 2, 512], F32)) for n in "ABCD")

        ident = sb("ident", [128, 128])
        ones = sb("ones", [128, 128])
        avg = sb("avg", [128, 128])
        before = sb("before", [P, P])
        same_expert = sb("same_expert", [128, 128])
        mod_i = sb("mod_i", [128, 128], I32)
        tile_row = sb("tile_row", [P, P])
        part_i = sb("part_i", [P, 3], I32)
        tile_col = sb("tile_col", [P, 1])
        slot_row = sb("slot_row", [P, CAP])
        slot_col = sb("slot_col", [128, SB])
        bit_table = sb("bit_table", [128, ROUNDS, 4], I32)
        eps_c = sb("eps_c", [128, 1])
        eps_t = sb("eps_t", [128, 1])
        zero_rows = sb("zero_rows", [P, TPI * C])
        prm = sb("prm", [128, 10])
        fold = sb("fold", [128, 12])
        taps_w = sb("taps_w", [128, 9])
        tap_diag = sb("tap_diag", [128, PE_TAPS, 128])
        pw_raw = sb("pw_raw", [128, 128])
        pw_T = sb("pw_T", [128, 128])
        pw_masked = sb("pw_masked", [128, 2, 128])
        wr_raw = sb("wr_raw", [128, E])
        wr_c = sb("wr_c", [128, E])
        b1_raw = sb("b1_raw", [E * FT, 128])
        b1_T = sb("b1_T", [128, E * FT])
        b2_raw = sb("b2_raw", [E, 128])
        b2_T = sb("b2_T", [128, E])
        x_in = sb("x_in", [128, 2, HW])
        x_res = sb("x_res", [128, 2, HW])
        x_pad = sb("x_pad", [128, 2, (H + 2) * PW])
        ln_tok = sb("ln_tok", [P, 2, TPI * C])
        ln_st = sb("ln_st", [P, TPI, 6])
        ln_sm = sb("ln_sm", [P, 7, TPI])
        row_st = sb("row_st", [P, TPI, 6])
        row_sm = sb("row_sm", [P, 7, TPI])
        conv = sb("conv", [128, 2, HW])
        act1 = sb("act1", [128, 2, HW])
        act2 = sb("act2", [128, 2, HW])
        limits = sb("limits", [128, 2])
        keep1 = sb("keep1", [128, 2])
        keep2 = sb("keep2", [128, 2])
        x1 = sb("x1", [128, 2, HW])
        x1_all = sb("x1_all", [128, N])
        rows = sb("rows", [P, 2, TPI * ROW])
        logits = sb("logits", [P, TILES * E])
        dist = sb("dist", [128, HW])
        junk = conv[:, :, :].rearrange("c q n -> c (q n)").bitcast(mybir.dt.bfloat16).rearrange("c (k n) -> c k n", n=HW)
        exps = sb("exps", [128, HW])
        zsum = sb("zsum", [128, 1])
        bmax = sb("bmax", [128, 2])
        mrow = sb("mrow", [1, 3, 128])
        mcol = sb("mcol", [128, 1])
        odd_dist = sb("odd_dist", [128, HW], I32)
        signs = sb("signs", [128, HW], mybir.dt.bfloat16)
        sign_sum = sb("sign_sum", [128, 1])
        half_same = sb("half_same", [128, 128])
        prefix = sb("prefix", [128, 1], I32)
        cand = sb("cand", [128, 4], I32)
        cnt = sb("cnt", [128, 4])
        kept = sb("kept", [128, 4])
        tcol = sb("tcol", [128, 4])
        bc = sb("bc", [128, 4, E])
        neg_max = sb("neg_max", [128, E])
        logits_T = sb("logits_T", [P, E * P])
        s_d = sb("s_d", [P, P])
        s_lt = sb("s_lt", [P, P])
        s_eq = sb("s_eq", [P, P])
        s_eqr = sb("s_eqr", [P, P])
        s_lim = sb("s_lim", [P, 1])
        s_tie = sb("s_tie", [P, P])
        s_sel = sb("s_sel", [P, P])
        s_rank = sb("s_rank", [P, P])
        s_edge = sb("s_edge", [P, 2])
        s_abs = sb("s_abs", [P, P + 1], F16)
        s_from = sb("s_from", [P, CAP], F16)
        s_in = sb("s_in", [P, CAP], F16)
        s_cmp = sb("s_cmp", [128, SB, P])
        s_p = sb("s_p", [128, SB])
        gather_idx = sb("gather_idx", [128, 2, SB], U32)
        scatter_idx = sb("scatter_idx", [128, 2, SB], U32)
        w1 = sb("w1", [128, 2, F])
        w2 = sb("w2", [128, 2, FT * C])
        picked = sb("picked", [128, 2, SB, ROW])
        picked_T = sb("picked_T", [128, CAP])
        hid = sb("hid", [128, FT, CAP])
        y_T = sb("y_T", [128, CAP])
        gate_e = sb("gate_e", [128, SB])
        gate = sb("gate", [128, SB])
        y_rows = sb("y_rows", [128, 2, SB, C])
        y_in, o_img = ln_tok, act2

        x_pad_v = x_pad[:, :, :].rearrange("c q (h w) -> c q h w", w=PW)
        ln_tiles = psA[0:P, :, :].rearrange("p a (t c) -> p (a t) c", c=C)
        row_tiles = psD[0:P, :, :].rearrange("p a (t c) -> p (a t) c", c=C)
        logit_ps = row_tiles[:, TPI, 0:TPI * E].rearrange("p (t e) -> p t e", e=E)

        s_prm, s_w = sem("params_loaded"), sem("weights_loaded")
        s_cz, s_const = sem("const_zeroed"), sem("consts_ready")
        s_setup, s_tiny, s_bnv, s_bns, s_wps, s_wsb = (sem(n) for n in (
            "setup_ready", "setup_math", "bn_var", "bn_std", "weights_turned", "weights_ready"))
        s_xin, s_xres = pair_of("x_in_loaded"), pair_of("x_res_loaded")
        s_t1, s_m1, s_mom1, s_std1, s_sc1, s_n1 = (sem(n) for n in (
            "ln_tokens", "ln_math", "ln_moments", "ln_std", "ln_scale", "ln_normed"))
        s_t2, s_pad, s_conv, s_taken, s_tap, s_h1, s_sg1, s_kp1, s_wm = (sem(n) for n in (
            "ln_channels", "padded", "conv_sums", "conv_taken", "taps_added", "act1_ready", "act1_signs", "keep1_ready", "pw_masked_ready"))
        s_pw, s_h2, s_sg2, s_kp2, s_x1, s_x1c = (sem(n) for n in (
            "pw_sums", "act2_ready", "act2_signs", "keep2_ready", "x1_ready", "x1_kept"))
        s_t3, s_m3, s_mom3, s_std3, s_sc3, s_n3, s_lg, s_rl = (sem(n) for n in (
            "row_tokens", "row_math", "row_moments", "row_std", "row_scale", "row_normed", "logits_ready", "row_logits"))
        s_rows = pair_of("rows_stored")
        s_yz = sem("y_zeroed")
        s_sp, s_sd, s_se, s_cand, s_cnt, s_tot, s_rnd = (sem(n) for n in (
            "search_turned", "search_math", "exps_summed", "candidates", "counted", "totals", "rounds"))
        s_ltt, s_ltc = sem("logits_turned"), sem("logits_T_ready")
        s_tie1, s_pm, s_cex, s_own, s_g, s_idx = (sem(n) for n in (
            "ties_before", "slot_math", "slots_before", "tile_ranks_ready", "slot_ranks", "slots_found"))
        s_gat, s_sca = [pair_of(f"rows_gathered_h{h}_") for h in range(2)], pair_of("rows_scattered")
        s_w1, s_w2 = pair_of("w1_loaded"), pair_of("w2_loaded")
        s_pt, s_ptc, s_l1, s_gelu, s_l2, s_yb, s_bt, s_yr = (sem(n) for n in (
            "picked_turned", "picked_T_ready", "hidden_sums", "hidden_ready", "out_sums", "out_biased", "out_turned", "out_rows"))
        s_ge, s_gt, s_si = sem("gate_exp"), sem("gate_ready"), sem("scatter_idx_ready")
        s_yl, s_fo = pair_of("y_loaded"), pair_of("out_stored")
        s_ft, s_fa = sem("final_turned"), sem("final_added")
        s_inv1, s_inv3, s_tapn, s_sdi, s_pd, s_odd, s_sgn = (sem(n) for n in (
            "ln_inverse", "row_inverse", "inner_taps", "search_inner", "slot_count", "odd_dist_ready", "signs_summed"))

        s_pool, s_act = sem("pool_past_waits"), sem("act_past_waits")

        block = ctx.enter_context(nc.Block())

        PM = 9

        @block.sync
        def _(sp):
            def load_x(img, q):
                sp.dma_start(x_in[:, q:q + 1, :], x_d[:, ds(img, 1), :]).then_inc(s_xin[q], 16)

            load_x(0, 0)
            for n, src in enumerate((bn1_g, bn1_b, bn1_m, bn1_v, bn2_g, bn2_b, bn2_m, bn2_v, dw_b, pw_b)):
                sp.dma_start(prm[:, n:n + 1], src.rearrange("(c a) -> c a", a=1)).then_inc(s_prm, 16)
            sp.dma_start(taps_w[:, :], dw_w.rearrange("c a h w -> c (a h w)")).then_inc(s_prm, 16)
            sp.dma_start(pw_raw[:, :], pw_w.rearrange("o c h w -> o (c h w)")).then_inc(s_w, 16)
            sp.dma_start(wr_raw[:, :], Wr).then_inc(s_w, 16)
            sp.dma_start(b1_raw[:, :], b1.rearrange("e (t f) -> (e t) f", f=128)).then_inc(s_w, 16)
            sp.dma_start(b2_raw[:, :], b2).then_inc(s_w, 16)

            def step(pair, u):
                on, img, q, use = image(pair, u, -1)
                if on:
                    if since(img, 2):
                        sp.wait_ge(s_t1, img - 1)
                    load_x(img, q)
                on, img, q, use = image(pair, u, 2)
                if on:
                    if since(img, 2):
                        sp.wait_ge(s_x1, img - 1)
                    sp.dma_start(x_res[:, q:q + 1, :], x_d[:, ds(img, 1), :]).then_inc(s_xres[q], 16)
                    if isinstance(img, int) and img == 0:
                        sp.wait_ge(s_const, 1)
                    sp.dma_start(y_t[:, ds(img, 1), :, :].rearrange("p i t c -> p (i t) c"),
                                 zero_rows[:, :].rearrange("p (t c) -> p t c", c=C)).then_inc(s_yz, 16)
                on, img, q, use = image(pair, u, 5)
                if on:
                    sp.wait_ge(s_rl, img + 1)
                    sp.wait_ge(s_n3, img + 1)
                    sp.dma_start(rows_t[:, ds(img, 1), :, :].rearrange("p i t c -> p (i t) c"),
                                 rows[:, q, :].rearrange("p (t c) -> p t c", c=ROW)).then_inc(s_rows[q], 16)

            steps(sp, step)

            def load_w(e, q):
                sp.dma_start(w1[:, q:q + 1, :], w1_d[:, ds(e, 1), :]).then_inc(s_w1[q], 16)
                sp.dma_start(w2[:, q, :].rearrange("p (t d) -> p t d", d=C),
                             w2_d[:, ds(e, 1), :, :].rearrange("p e t d -> p (e t) d")).then_inc(s_w2[q], 16)

            for q in range(2):
                load_w(q, q)
            with sp.Fori(0, E // 2 - 1) as pair:
                for q in range(2):
                    sp.wait_ge(s_l2, pair * 4 + 2 * q + 2)
                    load_w(pair * 2 + (q + 2), q)

            sp.wait_ge(s_sca[0], 16 * SB * E // 2)
            sp.wait_ge(s_sca[1], 16 * SB * E // 2)

            def load_y(img, q):
                sp.dma_start(y_in[:, q, :].rearrange("p (t c) -> p t c", c=C),
                             y_t[:, ds(img, 1), :, :].rearrange("p i t c -> p (i t) c")).then_inc(s_yl[q], 16)

            for q in range(2):
                load_y(q, q)
            with sp.Fori(0, B // 2 - 1) as pair:
                for q in range(2):
                    sp.wait_ge(s_ft, pair * 2 + q + 1)
                    load_y(pair * 2 + (q + 2), q)
            for q in range(2):
                sp.wait_ge(s_fo[q], 16 * B // 2)
                sp.wait_ge(s_rows[q], 16 * B // 2)

        @block.gpsimd
        def _(pool):
            nc.gpsimd.memset(ident[:, :], 0.0)
            nc.gpsimd.memset(ones[:, :], 1.0)
            nc.gpsimd.memset(avg[:, :], 1.0 / C)
            nc.gpsimd.memset(eps_c[:, :], LN_C_EPS)
            nc.gpsimd.memset(eps_t[:, :], LN_T_EPS)
            nc.gpsimd.memset(limits[:, 0:1], -DW_THRESH)
            nc.gpsimd.memset(limits[:, 1:2], -PW_THRESH)
            nc.gpsimd.memset(cnt[:, :], -OFFSET)
            nc.gpsimd.memset(prefix[:, :], 0)
            nc.gpsimd.memset(x_pad[:, :, :], 0.0)
            nc.gpsimd.memset(zero_rows[:, :], 0.0).then_inc(s_cz, 1)
            pool.wait_ge(s_cz, 1)
            nc.gpsimd.affine_select(out=ident[:, :], in_=ident[:, :], compare_op=ALU.not_equal, fill=1.0,
                                    base=0, pattern=[[-1, 128]], channel_multiplier=1)
            nc.gpsimd.iota(tile_row[:, :], pattern=[[1, TPI], [TPI, B]], base=0, channel_multiplier=0,
                           allow_small_or_imprecise_dtypes=True)
            nc.gpsimd.iota(part_i[:, 0:1], pattern=[[0, 1]], base=0, channel_multiplier=1)
            nc.gpsimd.iota(mod_i[:, :], pattern=[[-1, 128]], base=128, channel_multiplier=1)
            nc.gpsimd.iota(bit_table[:, :, :], pattern=[[0, ROUNDS], [1, 4]], base=0, channel_multiplier=0)
            nc.gpsimd.iota(slot_row[:, :], pattern=[[1, CAP]], base=0, channel_multiplier=0,
                           allow_small_or_imprecise_dtypes=True)
            nc.gpsimd.iota(slot_col[:, :], pattern=[[128, SB]], base=0, channel_multiplier=1,
                           allow_small_or_imprecise_dtypes=True).then_inc(s_const, 1)

            def step(pair, u):
                on, img, q, use = image(pair, u, 3)
                if on:
                    pool.wait_ge(s_x1, img + 1)
                    nc.gpsimd.tensor_copy(x1_all[:, ds(img * HW, HW)], x1[:, q, :]).then_inc(s_x1c, 1)

            steps(pool, step)

            def gather(e, q, use):
                pool.wait_ge(s_idx, e + 1)
                pool.sem_inc(s_pool, 1)
                for b in range(SB):
                    nc.gpsimd.indirect_dma_start(
                        out=picked[:, q, b, :], out_offset=None, in_=rows_dram,
                        in_offset=bass.IndirectOffsetOnAxis(ap=gather_idx[:, q, b:b + 1], axis=0),
                    ).then_inc(s_gat[b // 4][q], 16)

            def scatter(e, q, use):
                pool.wait_ge(s_si, e + 1)
                if q == 1 or since(e, 1):
                    pool.wait_ge(s_sca[1 - q], (use + q) * (16 * SB))
                for b in range(SB):
                    if b % 4 == 0:
                        pool.wait_ge(s_yr, e * 2 + (b // 4 + 1))
                        pool.sem_inc(s_pool, 1)
                    nc.gpsimd.indirect_dma_start(
                        out=y_dram, out_offset=bass.IndirectOffsetOnAxis(ap=scatter_idx[:, q, b:b + 1], axis=0),
                        in_=y_rows[:, q, b, :], in_offset=None, compute_op=ALU.add,
                    ).then_inc(s_sca[q], 16)

            for q in range(2):
                pool.wait_ge(s_rows[q], 16 * B // 2)
            pool.wait_ge(s_yz, 16 * B)
            for q in range(2):
                gather(q, q, 0)
            def gather_next(e, q):
                pool.wait_ge(s_pt, e * 2 + 2)
                pool.wait_ge(s_ge, e + 1)
                gather(e + 2, q, None)

            for q in range(2):
                gather_next(q, q)
                scatter(q, q, 0)
            with pool.Fori(1, E // 2 - 1) as pair:
                for q in range(2):
                    gather_next(pair * 2 + q, q)
                    scatter(pair * 2 + q, q, pair)
            for q in range(2):
                scatter(E - 2 + q, q, E // 2 - 1)

        @block.scalar
        def _(act):
            act.wait_ge(s_bnv, 1)
            nc.scalar.activation(fold[:, 2:4], fold[:, 0:2], ACT.Sqrt).then_inc(s_bns, 1)
            act.wait_ge(s_wps, 1)
            nc.scalar.activation(pw_T[:, :], psB[:, 0, 0:128], ACT.Copy)
            nc.scalar.activation(b1_T[:, :], psB[:, 0, 128:128 + E * FT], ACT.Copy)
            nc.scalar.activation(b2_T[:, :], psB[:, 0, 256:256 + E], ACT.Copy).then_inc(s_wsb, 1)
            act.wait_ge(s_setup, 1)
            act.wait_ge(s_const, 1)

            def step(pair, u):
                on2, img2, q2, _ = image(pair, u, 2)
                on3, img3, q3, _ = image(pair, u, 3)
                on, img, q, use = image(pair, u, 5)
                if on:
                    act.wait_ge(s_sc3, img + 1)
                    if since(img, 2):
                        act.wait_ge(s_rows[q], use * 16)
                    for t in range(TPI):
                        ins = nc.scalar.activation(rows[:, q, t * ROW:t * ROW + C], row_tiles[:, t, :], ACT.Identity,
                                                   bias=row_sm[:, 6, t:t + 1], scale=row_sm[:, 5, t:t + 1])
                    ins.then_inc(s_n3, 1)
                if on3:
                    if since(img3, 2):
                        act.wait_ge(s_x1, img3 - 1)
                    for h in range(2):
                        act.wait_ge(s_pw, img3 * 2 + h + 1)
                        nc.scalar.activation(act2[:, q3, h * HALF:(h + 1) * HALF], psB[:, h, 0:HALF], ACT.Relu,
                                             bias=fold[:, 9:10], scale=fold[:, 5:6]).then_inc(s_h2, 1)
                    if since(img3, 1):
                        act.wait_ge(s_kp2, img3)
                    if on2 and since(img2, 1):
                        act.wait_ge(s_sg1, img2)
                    act.wait_ge(s_h2, img3 * 2 + 2)
                    nc.scalar.activation(signs[:, :], act2[:, q3, :], ACT.Sign, bias=limits[:, 1:2],
                                         accum_out=keep2[:, 0:1]).then_inc(s_sg2, 1)
                on, img, q, use = image(pair, u, 0)
                if on:
                    act.wait_ge(s_mom1, img + 1)
                    nc.scalar.activation(ln_sm[:, 4, :], ln_sm[:, 3, :], ACT.Sqrt, bias=eps_c[0:P, :],
                                         scale=1.0 / C).then_inc(s_std1, 1)
                    act.wait_ge(s_sc1, img + 1)
                    if since(img, 2):
                        act.wait_ge(s_t2, img - 1)
                    for t in range(TPI):
                        ins = nc.scalar.activation(ln_tok[:, q, t * C:(t + 1) * C], ln_tiles[:, t, :], ACT.Identity,
                                                   bias=ln_sm[:, 6, t:t + 1], scale=ln_sm[:, 5, t:t + 1])
                    ins.then_inc(s_n1, 1)
                if on2:
                    act.wait_ge(s_tap, img2 + 1)
                    if since(img2, 2):
                        act.wait_ge(s_pw, img2 * 2 - 2)
                    nc.scalar.activation(act1[:, q2, :], conv[:, q2, :], ACT.Relu,
                                         bias=fold[:, 8:9], scale=fold[:, 4:5]).then_inc(s_h1, 1)
                    if since(img2, 1):
                        act.wait_ge(s_kp1, img2)
                    if on3:
                        act.wait_ge(s_sg2, img3 + 1)
                    act.wait_ge(s_h1, img2 + 1)
                    nc.scalar.activation(signs[:, :], act1[:, q2, :], ACT.Sign, bias=limits[:, 0:1],
                                         accum_out=keep1[:, 0:1]).then_inc(s_sg1, 1)
                on4, img4, _, _ = image(pair, u, 4)
                if on4:
                    act.wait_ge(s_mom3, img4 + 1)
                    nc.scalar.activation(row_sm[:, 4, :], row_sm[:, 3, :], ACT.Sqrt, bias=eps_t[0:P, :],
                                         scale=1.0 / C).then_inc(s_std3, 1)
                if on:
                    act.wait_ge(s_t2, img + 1)
                    if since(img, 2):
                        act.wait_ge(s_tap, img - 1)
                        act.wait_ge(s_conv, img * 2 - 2)
                    for a, (lo, n) in enumerate(((0, 16), (16, 12))):
                        ins = nc.scalar.activation(x_pad_v[:, q, 1 + lo:1 + lo + n, 1:1 + W],
                                                   psB[:, a, 0:n * W].rearrange("c (h w) -> c h w", w=W), ACT.Copy)
                    ins.then_inc(s_pad, 1)

            steps(act, step)

            def count_signs(r):
                act.wait_ge(s_cand, r * 3 + 1)
                nc.scalar.activation(signs[:, :], odd_dist[:, :].bitcast(F32), ACT.Sign, bias=cand[:, 3:4].bitcast(F32), scale=-1.0,
                                     accum_out=sign_sum[:, :]).then_inc(s_sgn, 1)

            act.wait_ge(s_sd, 3)
            nc.scalar.activation(exps[:, :], dist[:, :], ACT.Exp, scale=-1.0, accum_out=zsum[:, :]).then_inc(s_se, 1)
            for a in range(2):
                act.wait_ge(s_ltt, a + 1)
                nc.scalar.activation(logits_T[:, a * 4 * P:(a + 1) * 4 * P], psD[0:P, a, 0:4 * P],
                                     ACT.Copy).then_inc(s_ltc, 1)
            act.wait_ge(s_odd, 1)
            with act.Fori(0, (ROUNDS - 1) // UNROLL) as turn:
                for k in range(UNROLL):
                    count_signs(turn * UNROLL + k)

            def expert(e, q, use):
                for h in range(2):
                    act.wait_ge(s_gat[h][q], use * (8 * SB) + 8 * SB)
                if since(e, 1):
                    act.wait_ge(s_gt, e)
                act.sem_inc(s_act, 1)
                nc.scalar.activation(gate_e[:, :], picked[:, q, :, ds(C + e, 1)].rearrange("s b a -> s (b a)"),
                                     ACT.Exp, bias=neg_max[:, ds(e, 1)]).then_inc(s_ge, 1)
                for h in range(2):
                    act.wait_ge(s_pt, e * 2 + h + 1)
                    nc.scalar.activation(picked_T[:, h * HS:(h + 1) * HS], psA[:, h, :], ACT.Copy).then_inc(s_ptc, 1)
                for h in range(2):
                    for f in range(FT):
                        act.wait_ge(s_l1, e * (2 * FT) + (h * FT + f + 1))
                        act.sem_inc(s_act, 1)
                        nc.scalar.activation(hid[:, f, h * HS:(h + 1) * HS], psB[:, f % 2, :], ACT.Gelu,
                                             bias=b1_T[:, ds(e * FT + f, 1)]).then_inc(s_gelu, 1)

            act.wait_ge(s_sd, 9)
            for q in range(2):
                expert(q, q, 0)
            with act.Fori(1, E // 2) as pair:
                for q in range(2):
                    expert(pair * 2 + q, q, pair)

            with act.Fori(0, B // 2) as pair:
                for q in range(2):
                    act.wait_ge(s_fa, pair * 2 + q + 1)
                    act.dma_start(out_d[:, ds(pair * 2 + q, 1), :], o_img[:, q:q + 1, :]).then_inc(s_fo[q], 16)

        @block.tensor
        def _(pe):
            pe.wait_ge(s_const, 1)
            pe.wait_ge(s_w, 64)
            nc.tensor.transpose(psB[:, 0, 0:128], pw_raw[:, :], ident[:, :])
            nc.tensor.transpose(psB[:, 0, 128:128 + E * FT], b1_raw[:, :], ident[0:E * FT, 0:E * FT])
            nc.tensor.transpose(psB[:, 0, 256:256 + E], b2_raw[:, :], ident[0:E, 0:E])
            nc.tensor.matmul(psB[:, 0, 384:384 + E], avg[:, :], wr_raw[:, :], start=True, stop=True).then_inc(s_wps, 1)
            pe.wait_ge(s_setup, 1)
            pe.wait_ge(s_wsb, 1)

            def conv_half(img, q, h):
                for n in range(PE_TAPS):
                    dy, dx = TAPS[n]
                    y0 = h * LINES + dy
                    ins = nc.tensor.matmul(psC[:, h, 0:HALF].rearrange("c (h w) -> c h w", w=W), tap_diag[:, n, :],
                                           x_pad_v[:, q, y0:y0 + LINES, dx:dx + W],
                                           start=(n == 0), stop=(n == PE_TAPS - 1))
                ins.then_inc(s_conv, 1)

            def step(pair, u):
                on, img, q, use = image(pair, u, 0)
                if on:
                    pe.wait_ge(s_xin[q], use * 16 + 16)
                    if since(img, 1):
                        pe.wait_ge(s_n1, img)
                    for t in range(TPI):
                        ins = nc.tensor.transpose(ln_tiles[:, t, :], x_in[:, q, t * P:(t + 1) * P], ident[:, :])
                    ins.then_inc(s_t1, 1)
                on1, img1, q1, use1 = image(pair, u, 1)
                on3, img3, q, use = image(pair, u, 3)
                if on3:
                    pe.wait_ge(s_wm, img3 + 1)
                    if on1:
                        pe.wait_ge(s_pad, img1 + 1)
                    else:
                        pe.wait_ge(s_h2, img3 * 2)
                    for h in range(2):
                        nc.tensor.matmul(psB[:, h, 0:HALF], pw_masked[:, q, :], act1[:, q, h * HALF:(h + 1) * HALF],
                                         start=True, stop=True).then_inc(s_pw, 1)
                if on1:
                    pe.wait_ge(s_pad, img1 + 1)
                    if since(img1, 1):
                        pe.wait_ge(s_taken, img1)
                    conv_half(img1, q1, 0)
                on, img, q, use = image(pair, u, 4)
                if on:
                    if since(img, 1):
                        pe.wait_ge(s_n3, img)
                        pe.wait_ge(s_rl, img)
                    pe.wait_ge(s_x1, img + 1)
                    for t in range(TPI):
                        nc.tensor.transpose(row_tiles[:, t, :], x1[:, q, t * P:(t + 1) * P], ident[:, :])
                    for t in range(TPI):
                        ins = nc.tensor.matmul(logit_ps[:, t, :], x1[:, q, t * P:(t + 1) * P], wr_c[:, :],
                                               start=True, stop=True)
                    ins.then_inc(s_t3, 1)
                if on1:
                    conv_half(img1, q1, 1)
                on, img, q, use = image(pair, u, 0)
                if on:
                    pe.wait_ge(s_n1, img + 1)
                    if on3:
                        pe.wait_ge(s_h2, img3 * 2 + 2)
                    elif since(img, 1):
                        pe.wait_ge(s_pad, img)
                    for t in range(TPI):
                        ins = nc.tensor.transpose(psB[:, t // 4, (t % 4) * P:(t % 4 + 1) * P],
                                                  ln_tok[:, q, t * C:(t + 1) * C], ident[0:P, 0:P])
                    ins.then_inc(s_t2, 1)

            steps(pe, step)

            pe.wait_ge(s_n3, B)
            pe.wait_ge(s_rl, B)
            pe.wait_ge(s_h2, 2 * B)
            by_tile = logits[:, :].rearrange("p (t k) -> p t k", t=TPI)
            for t in range(TPI):
                ins = nc.tensor.transpose(psA[:, t // 4, (t % 4) * P:(t % 4 + 1) * P], by_tile[:, t, :], ident[0:P, 0:P])
            ins.then_inc(s_sp, 1)
            pe.wait_ge(s_sd, 1)
            nc.tensor.transpose(psB[0:1, 0, 0:128], bmax[:, 0:1], ident[:, :]).then_inc(s_sp, 1)
            pe.wait_ge(s_sd, 2)
            nc.tensor.transpose(psB[:, 0, 128:129], mrow[:, 2, :], ident[0:1, 0:1]).then_inc(s_sp, 1)
            by_expert = logits[:, :].rearrange("p (k e) -> p e k", e=E)
            for a in range(2):
                for e in range(4 * a, 4 * a + 4):
                    ins = nc.tensor.transpose(psD[0:P, a, (e % 4) * P:(e % 4 + 1) * P], by_expert[:, e, :], ident[0:P, 0:P])
                ins.then_inc(s_ltt, 1)
            pe.wait_ge(s_se, 1)
            nc.tensor.matmul(psB[:, 1, 0:1], same_expert[:, :], zsum[:, :], start=True, stop=True).then_inc(s_sp, 1)
            def totals(r, signed):
                pe.wait_ge(s_cnt, r + 1)
                ins = nc.tensor.matmul(psC[:, 0, 0:3 if signed else 4], same_expert[:, :], cnt[:, 0:3 if signed else 4],
                                       start=True, stop=True)
                if signed:
                    pe.wait_ge(s_sgn, r + 1)
                    ins = nc.tensor.matmul(psC[:, 0, 3:4], half_same[:, :], sign_sum[:, :], start=True, stop=True)
                ins.then_inc(s_tot, 1)

            with pe.Fori(0, (ROUNDS - 1) // UNROLL) as turn:
                for k in range(UNROLL):
                    totals(turn * UNROLL + k, True)
            totals(ROUNDS - 1, False)
            totals(ROUNDS, False)
            pe.wait_ge(s_sd, 7)
            for n in range(4):
                ins = nc.tensor.transpose(psB[:, 0, n * 128:(n + 1) * 128], tcol[:, n:n + 1].to_broadcast([128, 128]), ident[:, :])
            ins.then_inc(s_sp, 1)

            def ties(e):
                pe.wait_ge(s_pm, e * PM + 3)
                nc.tensor.matmul(psD[0:P, 0, 120:121], before[:, :], s_eqr[:, P - 1:P], start=True, stop=True).then_inc(s_tie1, 1)

            def slots_before(e):
                pe.wait_ge(s_pm, e * PM + 7)
                nc.tensor.matmul(psD[0:P, 0, 121:122], before[:, :], s_rank[:, P - 1:P], start=True, stop=True).then_inc(s_cex, 1)

            def slot_ranks(e):
                pe.wait_ge(s_own, e + 1)
                for b in range(SB):
                    ins = nc.tensor.matmul(psD[:, b // 4, (b % 4) * 128:(b % 4) * 128 + P + 1], s_in[:, b * 128:(b + 1) * 128],
                                           s_abs[:, :], start=True, stop=True)
                ins.then_inc(s_g, 1)

            pe.wait_ge(s_ltc, 2)
            for e in range(2):
                if e:
                    pe.wait_ge(s_idx, e)
                ties(e)
                slots_before(e)
                slot_ranks(e)

            def hidden(e, q, h):
                for f in range(FT):
                    n = h * FT + f
                    if n >= 2 or since(e, 1):
                        pe.wait_ge(s_gelu, e * (2 * FT) + n - 1)
                    nc.tensor.matmul(psB[:, f % 2, :], w1[:, q, f * 128:(f + 1) * 128], picked_T[:, h * HS:(h + 1) * HS],
                                     start=True, stop=True).then_inc(s_l1, 1)

            def down(e, q, h):
                pe.wait_ge(s_gelu, e * (2 * FT) + (h + 1) * FT)
                if since(e, 1):
                    pe.wait_ge(s_yb, e * 2 + h - 1)
                for f in range(FT):
                    ins = nc.tensor.matmul(psC[:, h, :], w2[:, q, f * C:(f + 1) * C], hid[:, f, h * HS:(h + 1) * HS],
                                           start=(f == 0), stop=(f == FT - 1))
                ins.then_inc(s_l2, 1)

            def back(e, h):
                pe.wait_ge(s_yb, e * 2 + h + 1)
                for b in range(4):
                    ins = nc.tensor.transpose(psA[:, h, b * 128:(b + 1) * 128], y_T[:, h * HS + b * 128:h * HS + (b + 1) * 128], ident[:, :])
                ins.then_inc(s_bt, 1)

            def expert(e, q, use, ahead):
                if since(e, 1):
                    pe.wait_ge(s_yr, e * 2)
                for h in range(2):
                    pe.wait_ge(s_gat[h][q], use * (8 * SB) + 8 * SB)
                    for b in range(4):
                        ins = nc.tensor.transpose(psA[:, h, b * 128:(b + 1) * 128], picked[:, q, h * 4 + b, 0:C], ident[:, :])
                    ins.then_inc(s_pt, 1)
                if ahead:
                    pe.wait_ge(s_idx, e + 2)
                    ties(e + 2)
                pe.wait_ge(s_w1[q], use * 16 + 16)
                pe.wait_ge(s_ptc, e * 2 + 1)
                hidden(e, q, 0)
                if ahead:
                    slots_before(e + 2)
                pe.wait_ge(s_ptc, e * 2 + 2)
                hidden(e, q, 1)
                if ahead:
                    slot_ranks(e + 2)
                pe.wait_ge(s_w2[q], use * 16 + 16)
                down(e, q, 0)
                down(e, q, 1)
                back(e, 0)
                back(e, 1)

            for q in range(2):
                expert(q, q, 0, True)
            with pe.Fori(1, E // 2 - 1) as pair:
                for q in range(2):
                    expert(pair * 2 + q, q, pair, True)
            for q in range(2):
                expert(E - 2 + q, q, E // 2 - 1, False)

            regions = (psB, psD)
            pe.wait_ge(s_gelu, E * 2 * FT)
            pe.wait_ge(s_idx, E)

            def turn_back(img, q, use):
                pe.wait_ge(s_yl[q], use * 16 + 16)
                if since(img, 2):
                    pe.wait_ge(s_fa, img - 1)
                for t in range(TPI):
                    ins = nc.tensor.transpose(regions[q][:, t // 4, (t % 4) * P:(t % 4 + 1) * P],
                                              y_in[:, q, t * C:(t + 1) * C], ident[0:P, 0:P])
                ins.then_inc(s_ft, 1)

            for q in range(2):
                turn_back(q, q, 0)
            with pe.Fori(1, B // 2) as pair:
                for q in range(2):
                    turn_back(pair * 2 + q, q, pair)

        @block.vector
        def _(dve):
            dve.wait_ge(s_prm, 16 * 11)
            pv = prm[:, 0:8].rearrange("c (n k) -> c k n", k=4)
            nc.vector.tensor_scalar(fold[:, 0:2], pv[:, 3, :], BN_EPS, None, ALU.add).then_inc(s_bnv, 1)
            nc.vector.tensor_tensor(fold[:, 6:8], prm[:, 8:10], pv[:, 2, :], ALU.subtract).then_inc(s_tiny, 1)
            dve.wait_ge(s_bns, 1)
            nc.vector.reciprocal(fold[:, 10:12], fold[:, 2:4]).then_inc(s_tiny, 1)
            dve.wait_ge(s_tiny, 2)
            nc.vector.tensor_tensor(fold[:, 4:6], fold[:, 10:12], pv[:, 0, :], ALU.mult).then_inc(s_tiny, 1)
            dve.wait_ge(s_tiny, 3)
            nc.vector.tensor_tensor(fold[:, 8:10], fold[:, 6:8], fold[:, 4:6], ALU.mult).then_inc(s_tiny, 1)
            dve.wait_ge(s_tiny, 4)
            nc.vector.tensor_tensor(fold[:, 8:10], fold[:, 8:10], pv[:, 1, :], ALU.add)
            dve.wait_ge(s_const, 1)
            for n in range(PE_TAPS):
                nc.vector.tensor_scalar(tap_diag[:, n, :], ident[:, :], taps_w[:, n:n + 1], None, ALU.mult)
            nc.vector.tensor_scalar(mod_i[:, :], mod_i[:, :], E - 1, None, ALU.bitwise_and).then_inc(s_tiny, 1)
            nc.vector.tensor_scalar(bit_table[:, ROUNDS - 1, :], bit_table[:, ROUNDS - 1, :], 1, None, ALU.min)
            for r in range(ROUNDS - 1):
                nc.vector.tensor_scalar(bit_table[:, r, :], bit_table[:, r, :], SHIFTS[r], None, ALU.logical_shift_left)
            nc.vector.tensor_scalar(part_i[:, 1:2], part_i[:, 0:1], B - 1, None, ALU.bitwise_and)
            nc.vector.tensor_scalar(part_i[:, 2:3], part_i[:, 0:1], 4, None, ALU.logical_shift_right).then_inc(s_tiny, 1)
            dve.wait_ge(s_tiny, 6)
            nc.vector.scalar_tensor_tensor(tile_col[:, :], part_i[:, 1:2], float(TPI), part_i[:, 2:3], ALU.mult, ALU.add)\
                .then_inc(s_tiny, 1)
            dve.wait_ge(s_tiny, 7)
            nc.vector.tensor_scalar(before[:, :], tile_row[:, :], tile_col[:, :], None, ALU.is_gt)
            nc.vector.tensor_copy(s_abs[:, P:P + 1], tile_col[:, :])
            nc.vector.tensor_scalar(same_expert[:, :], mod_i[:, :], 0, None, ALU.is_equal)
            nc.vector.tensor_scalar(half_same[:, :], mod_i[:, :], 0, 0.5, ALU.is_equal, ALU.mult)
            dve.wait_ge(s_wps, 1)
            dve.wait_ge(s_wsb, 1)
            nc.vector.tensor_tensor(wr_c[:, :], wr_raw[:, :], psB[:, 0, 384:384 + E], ALU.subtract).then_inc(s_setup, 1)

            def stats(tiles, st, s_math, img):
                for t in range(TPI):
                    ins = nc.vector.bn_stats(st[:, t, :], tiles[:, t, :])
                ins.then_inc(s_math, 1)

            def moments_a(st, sm, s_math, img):
                dve.wait_ge(s_math, img * 3 + 1)
                nc.vector.tensor_tensor(sm[:, 1, :], st[:, :, 1], st[:, :, 4], ALU.subtract)
                nc.vector.tensor_tensor(sm[:, 2, :], st[:, :, 2], st[:, :, 5], ALU.add)
                nc.vector.tensor_tensor(sm[:, 0, :], st[:, :, 1], st[:, :, 4], ALU.add).then_inc(s_math, 1)

            def moments_b(sm, s_math, img):
                dve.wait_ge(s_math, img * 3 + 2)
                nc.vector.scalar_tensor_tensor(sm[:, 1, :], sm[:, 1, :], C / 4.0, sm[:, 1, :], ALU.mult, ALU.mult)\
                    .then_inc(s_math, 1)

            def moments_c(sm, s_math, s_mom, img):
                dve.wait_ge(s_math, img * 3 + 3)
                nc.vector.tensor_tensor(sm[:, 3, :], sm[:, 1, :], sm[:, 2, :], ALU.add).then_inc(s_mom, 1)

            def inverse(sm, s_std, s_inv, img):
                dve.wait_ge(s_std, img + 1)
                nc.vector.reciprocal(sm[:, 5, :], sm[:, 4, :]).then_inc(s_inv, 1)

            def shift(sm, s_inv, s_sc, img):
                dve.wait_ge(s_inv, img + 1)
                nc.vector.scalar_tensor_tensor(sm[:, 6, :], sm[:, 0, :], -0.5, sm[:, 5, :], ALU.mult, ALU.mult)\
                    .then_inc(s_sc, 1)

            def tap(q, n, h, first):
                dy, dx = TAPS[PE_TAPS + n]
                y0, lines = (h * LINES, LINES) if first else (0, H)
                o = conv[:, q, y0 * W:(y0 + lines) * W].rearrange("c (h w) -> c h w", w=W)
                acc = psC[:, h, 0:HALF].rearrange("c (h w) -> c h w", w=W) if first else o
                return nc.vector.scalar_tensor_tensor(o, x_pad_v[:, q, y0 + dy:y0 + dy + lines, dx:dx + W],
                                                      taps_w[:, PE_TAPS + n:PE_TAPS + n + 1], acc, ALU.mult, ALU.add)

            def later_tap(img, q, n):
                if n == 1:
                    dve.wait_ge(s_taken, img + 1)
                else:
                    dve.wait_ge(s_tapn, img * (DVE_TAPS - 2) + n - 1)
                tap(q, n, 0, False).then_inc(s_tapn if n < DVE_TAPS - 1 else s_tap, 1)

            def step(pair, u):
                on0, img0, q0, _ = image(pair, u, 0)
                on2, img2, q2, _ = image(pair, u, 2)
                on3, img3, q3, use3 = image(pair, u, 3)
                on4, img4, q4, _ = image(pair, u, 4)
                on5, img5, q5, use5 = image(pair, u, 5)
                if on5:
                    inverse(row_sm, s_std3, s_inv3, img5)
                if on2:
                    dve.wait_ge(s_conv, img2 * 2 + 2)
                    if since(img2, 2):
                        dve.wait_ge(s_h1, img2 - 1)
                    tap(q2, 0, 0, True)
                if on5:
                    dve.wait_ge(s_inv3, img5 + 1)
                    inv = row_sm[:, 5, :].unsqueeze(2).to_broadcast([P, TPI, E])
                    lg = logits[:, :].rearrange("p (t k) -> p t k", t=TPI)[:, :, ds(img5 * E, E)]
                    nc.vector.tensor_tensor(lg, logit_ps, inv, ALU.mult)
                    if since(img5, 2):
                        dve.wait_ge(s_rows[q5], use5 * 16)
                    nc.vector.tensor_tensor(rows[:, q5, :].rearrange("p (t c) -> p t c", c=ROW)[:, :, C:ROW], logit_ps, inv,
                                            ALU.mult).then_inc(s_rl, 1)
                    dve.wait_ge(s_rl, img5 + 1)
                    shift(row_sm, s_inv3, s_sc3, img5)
                if on2:
                    tap(q2, 0, 1, True).then_inc(s_taken, 1)
                if on0:
                    dve.wait_ge(s_t1, img0 + 1)
                    stats(ln_tiles, ln_st, s_m1, img0)
                if on2 and DVE_TAPS > 1:
                    later_tap(img2, q2, 1)
                if on0:
                    moments_a(ln_st, ln_sm, s_m1, img0)
                if on3:
                    dve.wait_ge(s_sg2, img3 + 1)
                    nc.vector.tensor_scalar(keep2[:, 1:2], keep2[:, 0:1], 0.5 - HW, None, ALU.is_gt).then_inc(s_kp2, 1)
                if on0:
                    moments_b(ln_sm, s_m1, img0)
                if on2 and DVE_TAPS > 2:
                    later_tap(img2, q2, 2)
                if on0:
                    moments_c(ln_sm, s_m1, s_mom1, img0)
                if on3:
                    dve.wait_ge(s_kp2, img3 + 1)
                    dve.wait_ge(s_xres[q3], use3 * 16 + 16)
                    if since(img3, 2):
                        dve.wait_ge(s_t3, img3 - 1)
                        dve.wait_ge(s_x1c, img3 - 1)
                    nc.vector.scalar_tensor_tensor(x1[:, q3, :], act2[:, q3, :], keep2[:, 1:2], x_res[:, q3, :],
                                                   ALU.mult, ALU.add).then_inc(s_x1, 1)
                if on0:
                    inverse(ln_sm, s_std1, s_inv1, img0)
                    shift(ln_sm, s_inv1, s_sc1, img0)
                if on2 and DVE_TAPS > 3:
                    later_tap(img2, q2, 3)
                if on4:
                    dve.wait_ge(s_t3, img4 + 1)
                    stats(row_tiles, row_st, s_m3, img4)
                    moments_a(row_st, row_sm, s_m3, img4)
                    moments_b(row_sm, s_m3, img4)
                    moments_c(row_sm, s_m3, s_mom3, img4)
                if on2:
                    dve.wait_ge(s_sg1, img2 + 1)
                    nc.vector.tensor_scalar(keep1[:, 1:2], keep1[:, 0:1], 0.5 - HW, None, ALU.is_gt).then_inc(s_kp1, 1)
                    dve.wait_ge(s_kp1, img2 + 1)
                    if since(img2, 2):
                        dve.wait_ge(s_pw, img2 * 2 - 2)
                    if isinstance(img2, int) and img2 == 0:
                        dve.wait_ge(s_wsb, 1)
                    nc.vector.tensor_scalar(pw_masked[:, q2, :], pw_T[:, :], keep1[:, 1:2], None, ALU.mult).then_inc(s_wm, 1)

            steps(dve, step)

            la = psA[:, 0, 0:4 * P]
            lb = psA[:, 1, 0:3 * P]
            dve.wait_ge(s_sp, 1)
            nc.vector.reduce_max(bmax[:, 0:1], la, AX_X)
            nc.vector.reduce_max(bmax[:, 1:2], lb, AX_X).then_inc(s_sdi, 1)
            dve.wait_ge(s_sdi, 1)
            nc.vector.tensor_tensor(bmax[:, 0:1], bmax[:, 0:1], bmax[:, 1:2], ALU.max).then_inc(s_sd, 1)
            dve.wait_ge(s_sp, 2)
            nc.vector.tensor_reduce(mrow[:, 1, 0:E], psB[0:1, 0, 0:128].rearrange("a (i e) -> a e i", e=E), AX_X, ALU.max)\
                .then_inc(s_sdi, 1)
            dve.wait_ge(s_sdi, 2)
            nc.vector.tensor_copy(mrow[:, 2, :].rearrange("a (i e) -> a i e", e=E),
                                  mrow[:, 1, 0:E].unsqueeze(1).to_broadcast([1, B, E])).then_inc(s_sd, 1)
            dve.wait_ge(s_sp, 3)
            nc.vector.tensor_copy(mcol[:, :], psB[:, 0, 128:129]).then_inc(s_sdi, 1)
            dve.wait_ge(s_sdi, 3)
            nc.vector.tensor_scalar(dist[:, 0:4 * P], la, mcol[:, :], -1.0, ALU.subtract, ALU.mult)
            nc.vector.tensor_scalar(dist[:, 4 * P:HW], lb, mcol[:, :], -1.0, ALU.subtract, ALU.mult).then_inc(s_sd, 1)
            dve.wait_ge(s_sd, 3)
            nc.vector.tensor_scalar(odd_dist[:, :], dist[:, :].bitcast(I32), 1, None, ALU.bitwise_or).then_inc(s_odd, 1)

            def count(column, value):
                return nc.vector.tensor_scalar(junk[:, column, :], dist[:, :], value.bitcast(F32), -OFFSET, ALU.is_lt, ALU.add,
                                               accum_out=cnt[:, column:column + 1])

            def search_round(r, last):
                nc.vector.tensor_scalar(cand[:, :], bit_table[:, ds(r, 1), :].rearrange("p a b -> p (a b)"), prefix[:, :], None,
                                        ALU.bitwise_or).then_inc(s_cand, 1)
                dve.wait_ge(s_cand, r * 3 + 1)
                count(1, cand[:, 1:2])
                ins = count(2, cand[:, 2:3])
                if last:
                    ins = count(3, cand[:, 3:4])
                ins.then_inc(s_cnt, 1)
                dve.wait_ge(s_tot, r + 1)
                nc.vector.scalar_tensor_tensor(kept[:, :], psC[:, 0, 0:4], LIMIT, cand[:, :].bitcast(F32),
                                               ALU.is_lt, ALU.mult).then_inc(s_cand, 1)
                dve.wait_ge(s_cand, r * 3 + 2)
                nc.vector.reduce_max(prefix[:, :].bitcast(F32), kept[:, :], AX_X).then_inc(s_cand, 1)
                dve.wait_ge(s_cand, r * 3 + 3)

            with dve.Fori(0, (ROUNDS - 1) // UNROLL) as turn:
                for k in range(UNROLL):
                    search_round(turn * UNROLL + k, False)
            search_round(ROUNDS - 1, True)
            count(1, prefix[:, :]).then_inc(s_cnt, 1)
            nc.vector.tensor_copy(tcol[:, 0:1], prefix[:, :].bitcast(F32)).then_inc(s_sd, 1)
            nc.vector.tensor_copy(tcol[:, 2:3], mcol[:, :]).then_inc(s_sd, 1)
            dve.wait_ge(s_sp, 4)
            nc.vector.reciprocal(tcol[:, 3:4], psB[:, 1, 0:1]).then_inc(s_sd, 1)
            dve.wait_ge(s_tot, ROUNDS + 1)
            nc.vector.tensor_scalar(tcol[:, 1:2], psC[:, 0, 1:2], -1.0, LIMIT, ALU.mult, ALU.add).then_inc(s_sd, 1)
            dve.wait_ge(s_sp, 5)
            nc.vector.tensor_copy(bc[:, :, :], psB[:, 0, :].rearrange("p (n k) -> p n k", n=4)[:, :, 0:E]).then_inc(s_sd, 1)
            dve.wait_ge(s_sd, 8)
            nc.vector.tensor_scalar(neg_max[:, :], bc[:, 2, :], -1.0, None, ALU.mult).then_inc(s_sd, 1)
            dve.wait_ge(s_ltc, 2)

            def col(n, e):
                return bc[0:P, n, ds(e, 1)]

            def slots_a(e):
                nc.vector.tensor_scalar(s_d[:, :], logits_T[:, ds(e * P, P)], col(2, e), -1.0, ALU.subtract, ALU.mult)\
                    .then_inc(s_pm, 1)
                dve.wait_ge(s_pm, e * PM + 1)
                nc.vector.tensor_scalar(s_eq[:, :], s_d[:, :], col(0, e), None, ALU.is_equal).then_inc(s_pm, 1)
                nc.vector.tensor_scalar(s_lt[:, :], s_d[:, :], col(0, e), None, ALU.is_lt)
                dve.wait_ge(s_pm, e * PM + 2)
                nc.vector.tensor_tensor_scan(s_eqr[:, :], ones[0:P, 0:P], s_eq[:, :], 0.0, ALU.mult, ALU.add).then_inc(s_pm, 1)

            def slots_b(e):
                dve.wait_ge(s_tie1, e + 1)
                nc.vector.tensor_tensor(s_lim[:, :], col(1, e), psD[0:P, 0, 120:121], ALU.subtract).then_inc(s_pm, 1)
                dve.wait_ge(s_pm, e * PM + 4)
                nc.vector.scalar_tensor_tensor(s_tie[:, :], s_eqr[:, :], s_lim[:, :], s_eq[:, :], ALU.is_le, ALU.mult)\
                    .then_inc(s_pm, 1)
                dve.wait_ge(s_pm, e * PM + 5)
                nc.vector.tensor_tensor(s_sel[:, :], s_tie[:, :], s_lt[:, :], ALU.add).then_inc(s_pm, 1)
                dve.wait_ge(s_pm, e * PM + 6)
                nc.vector.tensor_tensor_scan(s_rank[:, :], ones[0:P, 0:P], s_sel[:, :], 0.0, ALU.mult, ALU.add).then_inc(s_pm, 1)

            def slots_c(e):
                dve.wait_ge(s_cex, e + 1)
                nc.vector.tensor_copy(s_edge[:, 0:1], psD[0:P, 0, 121:122])
                nc.vector.tensor_tensor(s_edge[:, 1:2], s_rank[:, P - 1:P], psD[0:P, 0, 121:122], ALU.add).then_inc(s_pm, 1)
                dve.wait_ge(s_pm, e * PM + 8)
                nc.vector.tensor_scalar(s_abs[:, 0:P], s_rank[:, :], s_edge[:, 0:1], None, ALU.add)
                nc.vector.tensor_scalar(s_from[:, :], slot_row[:, :], s_edge[:, 0:1], None, ALU.is_ge).then_inc(s_pm, 1)
                dve.wait_ge(s_pm, e * PM + 9)
                nc.vector.scalar_tensor_tensor(s_in[:, :], slot_row[:, :], s_edge[:, 1:2], s_from[:, :], ALU.is_lt, ALU.mult)\
                    .then_inc(s_own, 1)

            def slots_d(e, q, last_use):
                dve.wait_ge(s_g, e + 1)
                ranks = psD[:, :, :].rearrange("p a (b k) -> p (a b) k", k=128)
                nc.vector.tensor_tensor(s_cmp[:, :, :], ranks[:, :, 0:P], slot_col[:, :].unsqueeze(2).to_broadcast([128, SB, P]),
                                        ALU.is_le).then_inc(s_pd, 1)
                dve.wait_ge(s_pd, e * 2 + 1)
                nc.vector.reduce_sum(s_p[:, :], s_cmp[:, :, :], AX_X).then_inc(s_pd, 1)
                dve.wait_ge(s_pd, e * 2 + 2)
                if last_use is not None:
                    for h in range(2):
                        dve.wait_ge(s_gat[h][q], last_use * (8 * SB))
                nc.vector.scalar_tensor_tensor(gather_idx[:, q, :], ranks[:, :, P], float(P), s_p[:, :], ALU.mult, ALU.add)\
                    .then_inc(s_idx, 1)

            for e in range(2):
                slots_a(e)
                slots_b(e)
                slots_c(e)
                slots_d(e, e, None)

            def bias_out(e, h):
                dve.wait_ge(s_l2, e * 2 + h + 1)
                if since(e, 1):
                    dve.wait_ge(s_bt, e * 2 - 1 + h)
                nc.vector.tensor_scalar(y_T[:, h * HS:(h + 1) * HS], psC[:, h, :], b2_T[:, ds(e, 1)], None, ALU.add)\
                    .then_inc(s_yb, 1)

            def weigh(e, q, use, h):
                dve.wait_ge(s_bt, e * 2 + h + 1)
                if since(e, 2):
                    dve.wait_ge(s_sca[q], use * (16 * SB))
                nc.vector.tensor_tensor(y_rows[:, q, 4 * h:4 * h + 4, :], psA[:, h, :].rearrange("s (b d) -> s b d", d=C),
                                        gate[:, 4 * h:4 * h + 4].unsqueeze(2).to_broadcast([128, 4, C]), ALU.mult).then_inc(s_yr, 1)

            def expert(e, q, use, ahead):
                if since(e, 2):
                    dve.wait_ge(s_sca[q], use * (16 * SB))
                nc.vector.tensor_copy(scatter_idx[:, q, :], gather_idx[:, q, :]).then_inc(s_si, 1)
                dve.wait_ge(s_ge, e + 1)
                if since(e, 1):
                    dve.wait_ge(s_yr, e * 2)
                nc.vector.tensor_scalar(gate[:, :], gate_e[:, :], bc[:, 3, ds(e, 1)], None, ALU.mult).then_inc(s_gt, 1)
                if ahead:
                    slots_a(e + 2)
                    slots_b(e + 2)
                    slots_c(e + 2)
                    dve.wait_ge(s_si, e + 1)
                    slots_d(e + 2, q, use + 1)
                bias_out(e, 0)
                bias_out(e, 1)
                dve.wait_ge(s_gt, e + 1)
                weigh(e, q, use, 0)
                weigh(e, q, use, 1)

            for q in range(2):
                expert(q, q, 0, True)
            with dve.Fori(1, E // 2 - 1) as pair:
                for q in range(2):
                    expert(pair * 2 + q, q, pair, True)
            for q in range(2):
                expert(E - 2 + q, q, E // 2 - 1, False)

            regions = (psB, psD)

            dve.wait_ge(s_x1c, B)

            def add_up(img, q, use):
                dve.wait_ge(s_ft, img + 1)
                if since(img, 2):
                    dve.wait_ge(s_fo[q], use * 16)
                nc.vector.tensor_tensor(o_img[:, q, 0:4 * P], regions[q][:, 0, 0:4 * P], x1_all[:, ds(img * HW, 4 * P)], ALU.add)
                nc.vector.tensor_tensor(o_img[:, q, 4 * P:HW], regions[q][:, 1, 0:3 * P],
                                        x1_all[:, ds(img * HW + 4 * P, 3 * P)], ALU.add).then_inc(s_fa, 1)

            for q in range(2):
                add_up(q, q, 0)
            with dve.Fori(1, B // 2) as pair:
                for q in range(2):
                    add_up(pair * 2 + q, q, pair)


_INS = ['x', 'L0_conv_dw_w', 'L0_conv_dw_b', 'L0_conv_bn1_g', 'L0_conv_bn1_b', 'L0_conv_bn1_m', 'L0_conv_bn1_v',
        'L0_conv_pw_w', 'L0_conv_pw_b', 'L0_conv_bn2_g', 'L0_conv_bn2_b', 'L0_conv_bn2_m', 'L0_conv_bn2_v',
        'L0_ffn_Wr', 'L0_ffn_W1', 'L0_ffn_b1', 'L0_ffn_W2', 'L0_ffn_b2']
_OUTS = [((B, C, H, W), 'float32')]


def kernel(**inputs):
    import numpy as _np
    import concourse.bacc as _bacc
    from concourse import mybir as _mybir
    from concourse.bass_utils import run_bass_kernel_spmd as _run

    nc = _bacc.Bacc("TRN2", target_bir_lowering=False, num_devices=1)
    arrays, args = {}, []
    for name in _INS:
        a = _np.ascontiguousarray(inputs[name])
        arrays[f"in_{name}_dram"] = a
        args.append(nc.dram_tensor(f"in_{name}_dram", a.shape, _mybir.dt.from_np(a.dtype), kind="ExternalInput").ap())
    for i, (shape, dtype) in enumerate(_OUTS):
        dt = _mybir.dt.from_np(_np.dtype(dtype))
        args.append(nc.dram_tensor(f"out_{i}_dram", shape, dt, kind="ExternalOutput").ap())
    build(nc, *args)
    r = _run(nc, [arrays], core_ids=[0])
    got = tuple(r.results[0][f"out_{i}_dram"] for i in range(len(_OUTS)))
    return got[0]
```

```python
from contextlib import ExitStack

import concourse.bass as bass
from concourse import mybir

ALU = mybir.AluOpType
ACT = mybir.ActivationFunctionType
AX_X = mybir.AxisListType.X
F32 = mybir.dt.float32
F16 = mybir.dt.float16
I32 = mybir.dt.int32
U32 = mybir.dt.uint32
ds = bass.ds


B, C, H, W = 16, 128, 28, 28
HW = H * W
P = 112
TPI = HW // P
TILES = B * TPI
N = B * HW
E, F, CAP = 8, 512, 1024
SB = CAP // 128
FT = F // 128
ROW = C + E
HALF = HW // 2
LINES = H // 2
PW = W + 2
HS = CAP // 2
DW_THRESH, PW_THRESH = 4.0, 0.001
BN_EPS, LN_C_EPS, LN_T_EPS = 1e-5, 1e-6, 1e-5

BANK_TILES = (range(4), range(4, TPI))

PE_TAPS = 4
TAPS = [(dy, dx) for dy in range(3) for dx in range(3)]
DVE_TAPS = len(TAPS) - PE_TAPS

LOOP_FIRST, LOOP_END, LAST_PAIR = 3, B // 2 - 1, B // 2 + 3
ROUNDS = 16
OFFSET = HW / 2
LIMIT = float(CAP - B * OFFSET)
UNROLL = 5
ENDS = 4


def steps(eng, step):
    for pair in range(LOOP_FIRST):
        for u in range(2):
            step(pair, u)
    with eng.Fori(LOOP_FIRST, LOOP_END) as pair:
        for u in range(2):
            step(pair, u)
    for pair in range(LOOP_END, LAST_PAIR):
        for u in range(2):
            step(pair, u)


def image(pair, u, lag):
    o = u - lag
    img, use = pair * 2 + o, pair + o // 2
    active = not isinstance(pair, int) or 0 <= img < B
    return active, img, o % 2, use


def since(number, first):
    return not isinstance(number, int) or number >= first


def build(nc, x, dw_w, dw_b, bn1_g, bn1_b, bn1_m, bn1_v, pw_w, pw_b, bn2_g, bn2_b, bn2_m, bn2_v,
          Wr, W1, b1, W2, b2, out):
    x_d = x.rearrange("b c h w -> c b (h w)")
    out_d = out.rearrange("b c h w -> c b (h w)")
    w1_d = W1.rearrange("e d f -> d e f")
    w2_d = W2.rearrange("e (t p) d -> p e t d", p=128)

    with ExitStack() as ctx:
        def sb(name, shape, dt=F32):
            return ctx.enter_context(nc.sbuf_tensor(name, shape, dt))

        def sem(name):
            return ctx.enter_context(nc.semaphore(name))

        def pair_of(name):
            return [sem(f"{name}{q}") for q in range(2)]

        rows_dram = nc.dram_tensor("token_rows", (N, ROW), F32).ap()
        y_dram = nc.dram_tensor("moe_sum", (N, C), F32).ap()
        rows_t = rows_dram.rearrange("(i t p) c -> p i t c", p=P, t=TPI)
        y_t = y_dram.rearrange("(i t p) c -> p i t c", p=P, t=TPI)

        psA, psB, psC, psD = (ctx.enter_context(nc.psum_tensor(f"ps{n}", [128, 2, 512], F32)) for n in "ABCD")

        ident = sb("ident", [128, 128])
        ones = sb("ones", [128, 128])
        avg = sb("avg", [128, 128])
        before = sb("before", [P, P])
        same_expert = sb("same_expert", [128, 128])
        mod_i = sb("mod_i", [128, 128], I32)
        tile_row = sb("tile_row", [P, P])
        part_i = sb("part_i", [P, 3], I32)
        tile_col = sb("tile_col", [P, 1])
        slot_row = sb("slot_row", [P, CAP], F16)
        slot_col = sb("slot_col", [128, SB])
        round_bits = sb("round_bits", [128, 4], I32)
        eps_c = sb("eps_c", [128, 1])
        eps_t = sb("eps_t", [128, 1])
        warm = sb("warm", [128, 1])
        zero_rows = sb("zero_rows", [P, TPI * C])
        prm = sb("prm", [128, 10])
        fold = sb("fold", [128, 12])
        taps_w = sb("taps_w", [128, 9])
        tap_diag = sb("tap_diag", [128, PE_TAPS, 128])
        pw_raw = sb("pw_raw", [128, 128])
        pw_T = sb("pw_T", [128, 128])
        pw_masked = sb("pw_masked", [128, 2, 128])
        wr_raw = sb("wr_raw", [128, E])
        wr_c = sb("wr_c", [128, E])
        b1_raw = sb("b1_raw", [E * FT, 128])
        b1_T = sb("b1_T", [128, E * FT])
        b2_raw = sb("b2_raw", [E, 128])
        b2_T = sb("b2_T", [128, E])
        x_in = sb("x_in", [128, 2, HW])
        x_res = sb("x_res", [128, 2, HW])
        x_pad = sb("x_pad", [128, 2, (H + 2) * PW])
        ln_tok = sb("ln_tok", [P, 2, TPI * C])
        ln_st = sb("ln_st", [P, TPI, 6])
        ln_sm = sb("ln_sm", [P, 7, TPI])
        row_st = sb("row_st", [P, TPI, 6])
        row_sm = sb("row_sm", [P, 7, TPI])
        conv = sb("conv", [128, 2, HW])
        act1 = sb("act1", [128, 2, HW])
        act2 = sb("act2", [128, 2, HW])
        limits = sb("limits", [128, 2])
        keep1 = sb("keep1", [128, 2])
        keep2 = sb("keep2", [128, 2])
        x1 = sb("x1", [128, 2, HW])
        x1_all = sb("x1_all", [128, N])
        rows = sb("rows", [P, 2, TPI * ROW])
        logits = sb("logits", [P, TILES * E])
        dist = sb("dist", [128, HW])
        junk = conv[:, :, :].rearrange("c q n -> c (q n)").bitcast(mybir.dt.bfloat16).rearrange("c (k n) -> c k n", n=HW)
        exps = sb("exps", [128, HW])
        zsum = sb("zsum", [128, 1])
        bmax = sb("bmax", [128, 2])
        mrow = sb("mrow", [1, 3, 128])
        mcol = sb("mcol", [128, 1])
        odd_dist = sb("odd_dist", [128, HW], I32)
        signs = sb("signs", [128, HW], mybir.dt.bfloat16)
        signs2 = x_in[:, 0, 0:HALF // 2].bitcast(mybir.dt.bfloat16)
        sign_sum = sb("sign_sum", [128, 4], F16)
        same16 = sb("same16", [128, 128], F16)
        half_same = sb("half_same", [128, 128], F16)
        prefix = sb("prefix", [128, 1], I32)
        one_bit = sb("one_bit", [128, 2], I32)
        cand = sb("cand", [128, 4], I32)
        cnt = sb("cnt", [128, 4], F16)
        kept = sb("kept", [128, 4])
        tcol = sb("tcol", [128, 4])
        bc = sb("bc", [128, 4, E])
        neg_max = sb("neg_max", [128, E])
        logits_T = sb("logits_T", [P, E * P])
        s_d = sb("s_d", [P, P])
        s_lt = sb("s_lt", [P, P])
        s_eq = sb("s_eq", [P, P])
        s_eqr = sb("s_eqr", [P, P])
        s_lim = sb("s_lim", [P, 1])
        s_tie = sb("s_tie", [P, P])
        s_sel = sb("s_sel", [P, P])
        s_rank = sb("s_rank", [P, P])
        s_edge = sb("s_edge", [P, 2])
        s_abs = sb("s_abs", [P, P + 1], F16)
        s_from = sb("s_from", [P, CAP], F16)
        s_to = sb("s_to", [P, CAP], F16)
        s_in = sb("s_in", [P, CAP], F16)
        s_cmp = sb("s_cmp", [128, SB, P])
        s_p = sb("s_p", [128, SB])
        gather_idx = sb("gather_idx", [128, 2, SB], U32)
        scatter_idx = sb("scatter_idx", [128, 2, SB], U32)
        w1 = sb("w1", [128, 2, F])
        w2 = sb("w2", [128, 2, FT * C])
        picked = sb("picked", [128, 2, SB, ROW])
        picked_T = sb("picked_T", [128, CAP])
        hid = sb("hid", [128, FT, CAP])
        y_T = sb("y_T", [128, CAP])
        gate_e = sb("gate_e", [128, SB])
        gate = sb("gate", [128, SB])
        y_rows = sb("y_rows", [128, 2, SB, C])
        y_in = [ln_tok[:, 0, :], ln_tok[:, 1, :], x_pad[0:P, 0, 0:TPI * C], x_pad[0:P, 1, 0:TPI * C]]
        o_img = [act2[:, 0:1, :], act2[:, 1:2, :], act1[:, 0:1, :], act1[:, 1:2, :]]
        end_regions = (psB, psD, psA, psC)

        x_pad_v = x_pad[:, :, :].rearrange("c q (h w) -> c q h w", w=PW)
        ln_tiles = psA[0:P, :, :].rearrange("p a (t c) -> p (a t) c", c=C)
        row_tiles = psD[0:P, :, :].rearrange("p a (t c) -> p (a t) c", c=C)

        def row_region(img):
            return ln_tiles if isinstance(img, int) and img in (B - 3, B - 1) else row_tiles

        hidden_bank = [psB[:, 0, :], psB[:, 1, :], psC[:, 0, :], psC[:, 1, :]]

        def logit_region(img):
            return row_region(img)[:, TPI, 0:TPI * E].rearrange("p (t e) -> p t e", e=E)

        s_ident, s_avg = sem("ident_ready"), sem("avg_ready")
        s_prm, s_w = sem("params_loaded"), sem("weights_loaded")
        s_cz, s_const = sem("eps_ready"), sem("consts_ready")
        s_setup, s_tiny, s_bnv, s_bns, s_wps, s_wsb = (sem(n) for n in (
            "setup_ready", "setup_math", "bn_var", "bn_std", "weights_turned", "weights_ready"))
        s_xin, s_xres = pair_of("x_in_loaded"), pair_of("x_res_loaded")
        s_t1, s_m1, s_mom1, s_std1, s_sc1, s_n1 = (sem(n) for n in (
            "ln_tokens", "ln_math", "ln_moments", "ln_std", "ln_scale", "ln_normed"))
        s_t2, s_pad, s_conv, s_taken, s_tap, s_h1, s_sg1, s_kp1, s_wm = (sem(n) for n in (
            "ln_channels", "padded", "conv_sums", "conv_taken", "taps_added", "act1_ready", "act1_signs", "keep1_ready", "pw_masked_ready"))
        s_pw, s_h2, s_sg2, s_kp2, s_x1 = (sem(n) for n in (
            "pw_sums", "act2_ready", "act2_signs", "keep2_ready", "x1_ready"))
        s_x1c = pair_of("x1_kept")
        s_t3, s_m3, s_mom3, s_std3, s_sc3, s_n3, s_rl = (sem(n) for n in (
            "row_tokens", "row_math", "row_moments", "row_std", "row_scale", "row_normed", "row_logits"))
        s_rows = pair_of("rows_stored")
        s_yz = sem("y_zeroed")
        s_sp, s_sd, s_se, s_cand, s_cnt, s_tot = (sem(n) for n in (
            "search_turned", "search_math", "exps_summed", "candidates", "counted", "totals"))
        s_ltt, s_ltc = sem("logits_turned"), sem("logits_T_ready")
        s_tie1, s_pm, s_cex, s_own, s_g, s_idx = (sem(n) for n in (
            "ties_before", "slot_math", "slots_before", "tile_ranks_ready", "slot_ranks", "slots_found"))
        s_gat, s_sca = [pair_of(f"rows_gathered_h{h}_") for h in range(2)], pair_of("rows_scattered")
        s_w1, s_w2 = pair_of("w1_loaded"), pair_of("w2_loaded")
        s_pt, s_ptc, s_l1, s_gelu, s_l2, s_yb, s_bt, s_yr = (sem(n) for n in (
            "picked_turned", "picked_T_ready", "hidden_sums", "hidden_ready", "out_sums", "out_biased", "out_turned", "out_rows"))
        s_ge, s_gt, s_si = sem("gate_exp"), sem("gate_ready"), sem("scatter_idx_ready")
        s_yl, s_fo = ([sem(f"{name}{k}") for k in range(ENDS)] for name in ("y_loaded", "out_stored"))
        s_ft, s_fa = sem("final_turned"), sem("final_added")
        s_inv1, s_inv3, s_tapn, s_sdi, s_pd, s_odd, s_sgn = (sem(n) for n in (
            "ln_inverse", "row_inverse", "inner_taps", "search_inner", "slot_count", "odd_dist_ready", "signs_summed"))

        s_pool, s_act = sem("pool_past_waits"), sem("act_past_waits")

        ctx.enter_context(nc.allow_low_precision(reason="a partition's counts are whole numbers up to HW: fp16 holds them exactly"))
        block = ctx.enter_context(nc.Block())

        PM = 9

        @block.sync
        def _(sp):
            def load_x(img, q):
                sp.dma_start(x_in[:, q:q + 1, :], x_d[:, ds(img, 1), :]).then_inc(s_xin[q], 16)

            load_x(0, 0)
            for n, src in enumerate((bn1_g, bn1_b, bn1_m, bn1_v, bn2_g, bn2_b, bn2_m, bn2_v, dw_b, pw_b)):
                sp.dma_start(prm[:, n:n + 1], src.rearrange("(c a) -> c a", a=1)).then_inc(s_prm, 16)
            sp.dma_start(taps_w[:, :], dw_w.rearrange("c a h w -> c (a h w)")).then_inc(s_prm, 16)

            def step(pair, u):
                on, img, q, use = image(pair, u, -1)
                if on:
                    if since(img, 2):
                        sp.wait_ge(s_t1, img * 2 - 2)
                    load_x(img, q)
                on, img, q, use = image(pair, u, 2)
                if on:
                    if since(img, 2):
                        sp.wait_ge(s_x1, img - 1)
                    sp.dma_start(x_res[:, q:q + 1, :], x_d[:, ds(img, 1), :]).then_inc(s_xres[q], 16)
                    if isinstance(img, int) and img == 0:
                        sp.wait_ge(s_const, 1)
                    sp.dma_start(y_t[:, ds(img, 1), :, :].rearrange("p i t c -> p (i t) c"),
                                 zero_rows[:, :].rearrange("p (t c) -> p t c", c=C)).then_inc(s_yz, 16)
                on, img, q, use = image(pair, u, 5)
                if on:
                    sp.wait_ge(s_rl, img + 1)
                    sp.wait_ge(s_n3, img + 1)
                    sp.dma_start(rows_t[:, ds(img, 1), :, :].rearrange("p i t c -> p (i t) c"),
                                 rows[:, q, :].rearrange("p (t c) -> p t c", c=ROW)).then_inc(s_rows[q], 16)
                on, img, q, use = image(pair, u, 3)
                if on:
                    sp.wait_ge(s_x1, img + 1)
                    sp.dma_start(x1_all[:, ds(img * HW, HW)], x1[:, q, :]).then_inc(s_x1c[q], 16)

            steps(sp, step)

            def load_w(e, q):
                sp.dma_start(w1[:, q:q + 1, :], w1_d[:, ds(e, 1), :]).then_inc(s_w1[q], 16)
                sp.dma_start(w2[:, q, :].rearrange("p (t d) -> p t d", d=C),
                             w2_d[:, ds(e, 1), :, :].rearrange("p e t d -> p (e t) d")).then_inc(s_w2[q], 16)

            for q in range(2):
                load_w(q, q)
            with sp.Fori(0, E // 2 - 1) as pair:
                for q in range(2):
                    sp.wait_ge(s_l2, pair * 4 + 2 * q + 2)
                    load_w(pair * 2 + (q + 2), q)

            sp.wait_ge(s_sca[0], 16 * SB * E // 2)
            sp.wait_ge(s_sca[1], 16 * SB * E // 2)

            def load_y(img, k):
                sp.dma_start(y_in[k].rearrange("p (t c) -> p t c", c=C),
                             y_t[:, ds(img, 1), :, :].rearrange("p i t c -> p (i t) c")).then_inc(s_yl[k], 16)

            for k in range(ENDS):
                load_y(k, k)
            with sp.Fori(0, B // ENDS - 1) as turn:
                for k in range(ENDS):
                    sp.wait_ge(s_ft, turn * ENDS + k + 1)
                    load_y(turn * ENDS + (k + ENDS), k)
            for k in range(ENDS):
                sp.wait_ge(s_fo[k], 16 * B // ENDS)
            for q in range(2):
                sp.wait_ge(s_rows[q], 16 * B // 2)

        @block.gpsimd
        def _(pool):
            nc.gpsimd.memset(ident[:, :], 0.0)
            nc.gpsimd.memset(eps_c[:, :], LN_C_EPS)
            nc.gpsimd.memset(eps_t[:, :], LN_T_EPS).then_inc(s_cz, 1)
            pool.wait_ge(s_cz, 1)
            nc.gpsimd.affine_select(out=ident[:, :], in_=ident[:, :], compare_op=ALU.not_equal, fill=1.0,
                                    base=0, pattern=[[-1, 128]], channel_multiplier=1).then_inc(s_ident, 1)
            nc.gpsimd.memset(avg[:, :], 1.0 / C).then_inc(s_avg, 1)
            nc.gpsimd.memset(ones[:, :], 1.0)
            nc.gpsimd.memset(limits[:, 0:1], -DW_THRESH)
            nc.gpsimd.memset(limits[:, 1:2], -PW_THRESH)
            nc.gpsimd.memset(cnt[:, 0:3], -OFFSET)
            nc.gpsimd.memset(cnt[:, 3:4], 0.0)
            nc.gpsimd.memset(sign_sum[:, :], 0.0)
            nc.gpsimd.memset(prefix[:, :], 0)
            nc.gpsimd.memset(x_pad[:, :, :], 0.0)
            nc.gpsimd.memset(zero_rows[:, :], 0.0)
            nc.gpsimd.iota(tile_row[:, :], pattern=[[1, TPI], [TPI, B]], base=0, channel_multiplier=0,
                           allow_small_or_imprecise_dtypes=True)
            nc.gpsimd.iota(part_i[:, 0:1], pattern=[[0, 1]], base=0, channel_multiplier=1)
            nc.gpsimd.iota(mod_i[:, :], pattern=[[-1, 128]], base=128, channel_multiplier=1)
            nc.gpsimd.iota(one_bit[:, :], pattern=[[1, 2]], base=0, channel_multiplier=0)
            nc.gpsimd.iota(round_bits[:, :], pattern=[[1, 4]], base=0, channel_multiplier=0)
            nc.gpsimd.iota(slot_row[:, :], pattern=[[1, CAP]], base=0, channel_multiplier=0,
                           allow_small_or_imprecise_dtypes=True)
            nc.gpsimd.iota(slot_col[:, :], pattern=[[128, SB]], base=0, channel_multiplier=1,
                           allow_small_or_imprecise_dtypes=True).then_inc(s_const, 1)

            def gather(e, q, use):
                for b in range(SB):
                    if b % 4 == 0:
                        pool.wait_ge(s_idx, e * 2 + (b // 4 + 1))
                        pool.sem_inc(s_pool, 1)
                    nc.gpsimd.indirect_dma_start(
                        out=picked[:, q, b, :], out_offset=None, in_=rows_dram,
                        in_offset=bass.IndirectOffsetOnAxis(ap=gather_idx[:, q, b:b + 1], axis=0),
                    ).then_inc(s_gat[b // 4][q], 16)

            def scatter(e, q, use):
                pool.wait_ge(s_si, e + 1)
                if q == 1 or since(e, 1):
                    pool.wait_ge(s_sca[1 - q], (use + q) * (16 * SB))
                for b in range(SB):
                    if b % 4 == 0:
                        pool.wait_ge(s_yr, e * 2 + (b // 4 + 1))
                        pool.sem_inc(s_pool, 1)
                    nc.gpsimd.indirect_dma_start(
                        out=y_dram, out_offset=bass.IndirectOffsetOnAxis(ap=scatter_idx[:, q, b:b + 1], axis=0),
                        in_=y_rows[:, q, b, :], in_offset=None, compute_op=ALU.add,
                    ).then_inc(s_sca[q], 16)

            for q in range(2):
                pool.wait_ge(s_rows[q], 16 * B // 2)
            pool.wait_ge(s_yz, 16 * B)
            for q in range(2):
                gather(q, q, 0)

            def gather_next(e, q):
                pool.wait_ge(s_pt, e * 2 + 2)
                pool.wait_ge(s_ge, e + 1)
                gather(e + 2, q, None)

            for q in range(2):
                gather_next(q, q)
                scatter(q, q, 0)
            with pool.Fori(1, E // 2 - 1) as pair:
                for q in range(2):
                    gather_next(pair * 2 + q, q)
                    scatter(pair * 2 + q, q, pair)
            for q in range(2):
                scatter(E - 2 + q, q, E // 2 - 1)

        @block.scalar
        def _(act):
            act.dma_start(pw_raw[:, :], pw_w.rearrange("o c h w -> o (c h w)")).then_inc(s_w, 16)
            act.dma_start(wr_raw[:, :], Wr).then_inc(s_w, 16)
            act.dma_start(b1_raw[:, :], b1.rearrange("e (t f) -> (e t) f", f=128)).then_inc(s_w, 16)
            act.dma_start(b2_raw[:, :], b2).then_inc(s_w, 16)

            def step(pair, u):
                on2, img2, q2, _ = image(pair, u, 2)
                on3, img3, q3, _ = image(pair, u, 3)
                on5, img5, q5, use5 = image(pair, u, 5)
                on, img, q, use = image(pair, u, 0)

                def norm_rows():
                    act.wait_ge(s_sc3, img5 + 1)
                    if since(img5, 2):
                        act.wait_ge(s_rows[q5], use5 * 16)
                    for t in range(TPI):
                        ins = nc.scalar.activation(rows[:, q5, t * ROW:t * ROW + C], row_region(img5)[:, t, :], ACT.Identity,
                                                   bias=row_sm[:, 6, t:t + 1], scale=row_sm[:, 5, t:t + 1])
                    ins.then_inc(s_n3, 1)

                def second_activation():
                    if since(img3, 2):
                        act.wait_ge(s_x1, img3 - 1)
                    for h in range(2):
                        act.wait_ge(s_pw, img3 * 2 + h + 1)
                        nc.scalar.activation(act2[:, q3, h * HALF:(h + 1) * HALF], psB[:, h, 0:HALF], ACT.Relu,
                                             bias=fold[:, 9:10], scale=fold[:, 5:6]).then_inc(s_h2, 1)
                    if since(img3, 1):
                        act.wait_ge(s_kp2, img3)
                    if on2 and since(img2, 1):
                        act.wait_ge(s_sg1, img2)
                    act.wait_ge(s_h2, img3 * 2 + 2)
                    nc.scalar.activation(signs[:, :], act2[:, q3, :], ACT.Sign, bias=limits[:, 1:2],
                                         accum_out=keep2[:, 0:1]).then_inc(s_sg2, 1)

                def first_signs():
                    if since(img2, 1):
                        act.wait_ge(s_kp1, img2)
                    if on3:
                        act.wait_ge(s_sg2, img3 + 1)
                    act.wait_ge(s_h1, img2 + 1)
                    nc.scalar.activation(signs[:, :], act1[:, q2, :], ACT.Sign, bias=limits[:, 0:1],
                                         accum_out=keep1[:, 0:1]).then_inc(s_sg1, 1)

                ending = not image(pair, u, 1)[0]
                if ending and on3:
                    second_activation()
                if on5:
                    norm_rows()
                if on:
                    if isinstance(img, int) and img == 0:
                        act.wait_ge(s_cz, 1)
                    act.wait_ge(s_mom1, img + 1)
                    nc.scalar.activation(ln_sm[:, 4, :], ln_sm[:, 3, :], ACT.Sqrt, bias=eps_c[0:P, :],
                                         scale=1.0 / C).then_inc(s_std1, 1)
                    if isinstance(img, int) and img == 0:
                        act.wait_ge(s_bnv, 1)
                        nc.scalar.activation(fold[:, 2:4], fold[:, 0:2], ACT.Sqrt).then_inc(s_bns, 1)
                if on3 and not ending:
                    second_activation()
                if on:
                    act.wait_ge(s_sc1, img + 1)
                    if since(img, 2):
                        act.wait_ge(s_t2, img * 2 - 2)
                    for tiles in BANK_TILES:
                        for t in tiles:
                            ins = nc.scalar.activation(ln_tok[:, q, t * C:(t + 1) * C], ln_tiles[:, t, :], ACT.Identity,
                                                       bias=ln_sm[:, 6, t:t + 1], scale=ln_sm[:, 5, t:t + 1])
                        ins.then_inc(s_n1, 1)
                    if isinstance(img, int) and img == 0:
                        act.wait_ge(s_wps, 1)
                        nc.scalar.activation(pw_T[:, :], psB[:, 0, 0:128], ACT.Copy)
                        nc.scalar.activation(b1_T[:, :], psB[:, 0, 128:128 + E * FT], ACT.Copy)
                        nc.scalar.activation(b2_T[:, :], psB[:, 0, 256:256 + E], ACT.Copy).then_inc(s_wsb, 1)
                if on2:
                    if isinstance(img2, int) and img2 == 0:
                        act.wait_ge(s_setup, 1)
                    act.wait_ge(s_tap, img2 + 1)
                    if since(img2, 2):
                        act.wait_ge(s_pw, img2 * 2 - 2)
                    nc.scalar.activation(act1[:, q2, :], conv[:, q2, :], ACT.Relu,
                                         bias=fold[:, 8:9], scale=fold[:, 4:5]).then_inc(s_h1, 1)
                if on2 and ending:
                    first_signs()
                on4, img4, _, _ = image(pair, u, 4)
                if on4:
                    act.wait_ge(s_mom3, img4 + 1)
                    nc.scalar.activation(row_sm[:, 4, :], row_sm[:, 3, :], ACT.Sqrt, bias=eps_t[0:P, :],
                                         scale=1.0 / C).then_inc(s_std3, 1)
                if on:
                    if isinstance(img, int) and img == 0:
                        act.wait_ge(s_const, 1)
                    if since(img, 2):
                        act.wait_ge(s_tap, img - 1)
                        act.wait_ge(s_conv, img * 2 - 2)
                    for a, (lo, n) in enumerate(((0, 16), (16, 12))):
                        act.wait_ge(s_t2, img * 2 + a + 1)
                        nc.scalar.activation(x_pad_v[:, q, 1 + lo:1 + lo + n, 1:1 + W],
                                             psB[:, a, 0:n * W].rearrange("c (h w) -> c h w", w=W), ACT.Copy).then_inc(s_pad, 1)
                if on2 and not ending:
                    first_signs()

            steps(act, step)

            def count_signs(r):
                act.wait_ge(s_cand, r * 3 + 1)
                for column, lo in ((3, 0), (2, HALF)):
                    ins = nc.scalar.activation(signs[:, lo:HW] if column == 3 else signs2[:, :], odd_dist[:, lo:HW].bitcast(F32),
                                               ACT.Sign, bias=cand[:, column:column + 1].bitcast(F32), scale=-1.0,
                                               accum_out=sign_sum[:, column:column + 1])
                ins.then_inc(s_sgn, 1)

            act.wait_ge(s_sd, 3)
            nc.scalar.activation(exps[:, :], dist[:, :], ACT.Exp, scale=-1.0, accum_out=zsum[:, :]).then_inc(s_se, 1)
            for a in range(2):
                act.wait_ge(s_ltt, a + 1)
                nc.scalar.activation(logits_T[:, a * 4 * P:(a + 1) * 4 * P], psD[0:P, a, 0:4 * P],
                                     ACT.Copy).then_inc(s_ltc, 1)
            act.wait_ge(s_odd, 1)
            with act.Fori(0, (ROUNDS - 1) // UNROLL) as turn:
                for k in range(UNROLL):
                    count_signs(turn * UNROLL + k)

            def take_turned(e, h):
                act.wait_ge(s_pt, e * 2 + h + 1)
                nc.scalar.activation(picked_T[:, h * HS:(h + 1) * HS], psA[:, h, :], ACT.Copy).then_inc(s_ptc, 1)

            def gate_exps(e, q, use):
                for h in range(2):
                    act.wait_ge(s_gat[h][q], use * (8 * SB) + 8 * SB)
                if since(e, 1):
                    act.wait_ge(s_gt, e)
                act.sem_inc(s_act, 1)
                nc.scalar.activation(gate_e[:, :], picked[:, q, :, ds(C + e, 1)].rearrange("s b a -> s (b a)"),
                                     ACT.Exp, bias=neg_max[:, ds(e, 1)]).then_inc(s_ge, 1)

            def load_gelu():
                nc.scalar.activation(warm[:, :], eps_c[:, :], ACT.Gelu)

            def gelus(e, h):
                for f in range(FT):
                    act.wait_ge(s_l1, e * (2 * FT) + (h * FT + f + 1))
                    act.sem_inc(s_act, 1)
                    nc.scalar.activation(hid[:, f, h * HS:(h + 1) * HS], hidden_bank[f], ACT.Gelu,
                                         bias=b1_T[:, ds(e * FT + f, 1)]).then_inc(s_gelu, 1)

            def expert(e, q, use, another):
                for h in range(2):
                    if isinstance(e, int) and e == 0:
                        take_turned(e, h)
                    gelus(e, h)
                if isinstance(e, int) and e == 0:
                    gate_exps(e, q, use)
                if another:
                    for h in range(2):
                        take_turned(e + 1, h)
                    gate_exps(e + 1, 1 - q, use + q)
                    load_gelu()

            load_gelu()
            act.wait_ge(s_sd, 9)
            for q in range(2):
                expert(q, q, 0, True)
            with act.Fori(1, E // 2 - 1) as pair:
                for q in range(2):
                    expert(pair * 2 + q, q, pair, True)
            for q in range(2):
                expert(E - 2 + q, q, E // 2 - 1, q == 0)

            with act.Fori(0, B // ENDS) as turn:
                for k in range(ENDS):
                    act.wait_ge(s_fa, turn * ENDS + k + 1)
                    act.dma_start(out_d[:, ds(turn * ENDS + k, 1), :], o_img[k]).then_inc(s_fo[k], 16)

        @block.tensor
        def _(pe):
            pe.wait_ge(s_ident, 1)

            def turn_weights():
                pe.wait_ge(s_avg, 1)
                pe.wait_ge(s_w, 64)
                nc.tensor.transpose(psB[:, 0, 0:128], pw_raw[:, :], ident[:, :])
                nc.tensor.transpose(psB[:, 0, 128:128 + E * FT], b1_raw[:, :], ident[0:E * FT, 0:E * FT])
                nc.tensor.transpose(psB[:, 0, 256:256 + E], b2_raw[:, :], ident[0:E, 0:E])
                nc.tensor.matmul(psB[:, 0, 384:384 + E], avg[:, :], wr_raw[:, :], start=True, stop=True).then_inc(s_wps, 1)

            def conv_half(img, q, h):
                if since(img, 1):
                    pe.wait_ge(s_taken, img * 2 + h - 1)
                for n in range(PE_TAPS):
                    dy, dx = TAPS[n]
                    y0 = h * LINES + dy
                    ins = nc.tensor.matmul(psC[:, h, 0:HALF].rearrange("c (h w) -> c h w", w=W), tap_diag[:, n, :],
                                           x_pad_v[:, q, y0:y0 + LINES, dx:dx + W],
                                           start=(n == 0), stop=(n == PE_TAPS - 1))
                ins.then_inc(s_conv, 1)

            def step(pair, u):
                on, img, q, use = image(pair, u, 0)
                if on:
                    pe.wait_ge(s_xin[q], use * 16 + 16)
                    for a, tiles in enumerate(BANK_TILES):
                        if since(img, 1):
                            pe.wait_ge(s_n1, img * 2 + a - 1)
                        for t in tiles:
                            ins = nc.tensor.transpose(ln_tiles[:, t, :], x_in[:, q, t * P:(t + 1) * P], ident[:, :])
                        ins.then_inc(s_t1, 1)
                    if isinstance(img, int) and img == 0:
                        turn_weights()
                on1, img1, q1, use1 = image(pair, u, 1)
                on3, img3, q, use = image(pair, u, 3)
                if on1:
                    if isinstance(img1, int) and img1 == 0:
                        pe.wait_ge(s_setup, 1)
                    pe.wait_ge(s_pad, img1 * 2 + 1)
                    conv_half(img1, q1, 0)
                if on3:
                    pe.wait_ge(s_wm, img3 + 1)
                    if on1:
                        pe.wait_ge(s_pad, img1 * 2 + 2)
                    else:
                        pe.wait_ge(s_h2, img3 * 2)
                    for h in range(2):
                        nc.tensor.matmul(psB[:, h, 0:HALF], pw_masked[:, q, :], act1[:, q, h * HALF:(h + 1) * HALF],
                                         start=True, stop=True).then_inc(s_pw, 1)
                on, img, q, use = image(pair, u, 4)
                if on:
                    if isinstance(img, int) and img == B - 3:
                        pe.wait_ge(s_n1, B * 2)
                    elif since(img, 1):
                        before_it = img - 1 if isinstance(img, int) and img > B - 3 else img
                        pe.wait_ge(s_n3, before_it)
                        pe.wait_ge(s_rl, before_it)
                    pe.wait_ge(s_x1, img + 1)
                    for t in range(TPI):
                        ins = nc.tensor.transpose(row_region(img)[:, t, :], x1[:, q, t * P:(t + 1) * P], ident[:, :])
                        if t == BANK_TILES[0][-1]:
                            ins.then_inc(s_t3, 1)
                    for t in range(TPI):
                        ins = nc.tensor.matmul(logit_region(img)[:, t, :], x1[:, q, t * P:(t + 1) * P], wr_c[:, :],
                                               start=True, stop=True)
                    ins.then_inc(s_t3, 1)
                if on1:
                    pe.wait_ge(s_pad, img1 * 2 + 2)
                    conv_half(img1, q1, 1)
                on, img, q, use = image(pair, u, 0)
                if on:
                    if on3:
                        pe.wait_ge(s_h2, img3 * 2 + 2)
                    elif since(img, 1):
                        pe.wait_ge(s_pad, img * 2)
                    else:
                        pe.wait_ge(s_setup, 1)
                    for a, tiles in enumerate(BANK_TILES):
                        pe.wait_ge(s_n1, img * 2 + a + 1)
                        for t in tiles:
                            ins = nc.tensor.transpose(psB[:, a, (t % 4) * P:(t % 4 + 1) * P],
                                                      ln_tok[:, q, t * C:(t + 1) * C], ident[0:P, 0:P])
                        ins.then_inc(s_t2, 1)

            steps(pe, step)

            pe.wait_ge(s_rl, B)
            pe.wait_ge(s_taken, 2 * B)
            pe.wait_ge(s_h2, 2 * B)
            by_tile = logits[:, :].rearrange("p (t k) -> p t k", t=TPI)
            for t in range(TPI):
                ins = nc.tensor.transpose(psC[:, t // 4, (t % 4) * P:(t % 4 + 1) * P], by_tile[:, t, :], ident[0:P, 0:P])
            ins.then_inc(s_sp, 1)
            pe.wait_ge(s_sd, 1)
            nc.tensor.transpose(psB[0:1, 0, 0:128], bmax[:, 0:1], ident[:, :]).then_inc(s_sp, 1)
            pe.wait_ge(s_sd, 2)
            nc.tensor.transpose(psB[:, 0, 128:129], mrow[:, 2, :], ident[0:1, 0:1]).then_inc(s_sp, 1)
            pe.wait_ge(s_n3, B)
            by_expert = logits[:, :].rearrange("p (k e) -> p e k", e=E)
            for a in range(2):
                for e in range(4 * a, 4 * a + 4):
                    ins = nc.tensor.transpose(psD[0:P, a, (e % 4) * P:(e % 4 + 1) * P], by_expert[:, e, :], ident[0:P, 0:P])
                ins.then_inc(s_ltt, 1)
            pe.wait_ge(s_se, 1)
            nc.tensor.matmul(psB[:, 1, 0:1], same_expert[:, :], zsum[:, :], start=True, stop=True).then_inc(s_sp, 1)

            def totals(r, signed):
                if signed:
                    pe.wait_ge(s_sgn, r + 1)
                    nc.tensor.matmul(psA[:, 0, 0:4], half_same[:, :], sign_sum[:, :], start=True, stop=False)
                pe.wait_ge(s_cnt, r + 1)
                columns = 4 if signed else 2
                nc.tensor.matmul(psA[:, 0, 0:columns], same16[:, :], cnt[:, 0:columns], start=not signed, stop=True)\
                    .then_inc(s_tot, 1)

            with pe.Fori(0, (ROUNDS - 1) // UNROLL) as turn:
                for k in range(UNROLL):
                    totals(turn * UNROLL + k, True)
            totals(ROUNDS - 1, False)
            totals(ROUNDS, False)
            pe.wait_ge(s_sd, 7)
            for n in range(4):
                ins = nc.tensor.transpose(psB[:, 0, n * 128:(n + 1) * 128], tcol[:, n:n + 1].to_broadcast([128, 128]), ident[:, :])
            ins.then_inc(s_sp, 1)

            def ties(e):
                pe.wait_ge(s_pm, e * PM + 3)
                nc.tensor.matmul(psD[0:P, 0, 120:121], before[:, :], s_eqr[:, P - 1:P], start=True, stop=True).then_inc(s_tie1, 1)

            def slots_before(e):
                pe.wait_ge(s_pm, e * PM + 7)
                nc.tensor.matmul(psD[0:P, 0, 121:122], before[:, :], s_rank[:, P - 1:P], start=True, stop=True).then_inc(s_cex, 1)

            def slot_ranks(e):
                pe.wait_ge(s_own, e + 1)
                for b in range(SB):
                    ins = nc.tensor.matmul(psD[:, b // 4, (b % 4) * 128:(b % 4) * 128 + P + 1], s_in[:, b * 128:(b + 1) * 128],
                                           s_abs[:, :], start=True, stop=True)
                    if b % 4 == 3:
                        ins.then_inc(s_g, 1)

            def turn_picked(e, q, use, h):
                if since(e, 2):
                    pe.wait_ge(s_yr, e * 2 - 2)
                pe.wait_ge(s_gat[h][q], use * (8 * SB) + 8 * SB)
                for b in range(4):
                    ins = nc.tensor.transpose(psA[:, h, b * 128:(b + 1) * 128], picked[:, q, h * 4 + b, 0:C], ident[:, :])
                ins.then_inc(s_pt, 1)

            pe.wait_ge(s_ltc, 2)
            for e in range(2):
                if e:
                    pe.wait_ge(s_idx, e * 2)
                ties(e)
                slots_before(e)
                if e:
                    turn_picked(0, 0, 0, 0)
                slot_ranks(e)

            def hidden(e, q, h, after):
                pe.wait_ge(s_ptc, e * 2 + h + 1)
                for f in range(FT):
                    if h == 1:
                        pe.wait_ge(s_gelu, e * (2 * FT) + f + 1)
                    elif since(e, 1):
                        if f < 2:
                            pe.wait_ge(s_gelu, e * (2 * FT) + f - 3)
                        else:
                            pe.wait_ge(s_yb, e * 4 + 2 * f - 6)
                    nc.tensor.matmul(hidden_bank[f], w1[:, q, f * 128:(f + 1) * 128], picked_T[:, h * HS:(h + 1) * HS],
                                     start=True, stop=True).then_inc(s_l1, 1)
                    if f in after:
                        after[f](e + 2)

            def down(e, q, h):
                pe.wait_ge(s_gelu, e * (2 * FT) + (FT + 3 + h))
                for f in range(FT):
                    ins = nc.tensor.matmul(psC[:, h, :], w2[:, q, f * C:(f + 1) * C], hid[:, f, h * HS:(h + 1) * HS],
                                           start=(f == 0), stop=(f == FT - 1))
                ins.then_inc(s_l2, 1)

            def back(e, h, another):
                if another:
                    pe.wait_ge(s_ptc, e * 2 + h + 3)
                for b in range(4):
                    if b % 2 == 0:
                        pe.wait_ge(s_yb, e * 4 + (2 * h + b // 2 + 1))
                    ins = nc.tensor.transpose(psA[:, h, b * 128:(b + 1) * 128], y_T[:, h * HS + b * 128:h * HS + (b + 1) * 128], ident[:, :])
                ins.then_inc(s_bt, 1)

            def first_ties(e):
                pe.wait_ge(s_idx, e * 2)
                ties(e)

            def expert(e, q, use, ahead, another):
                pe.wait_ge(s_w1[q], use * 16 + 16)
                for h in range(2):
                    if isinstance(e, int) and e == 0 and h == 1:
                        turn_picked(e, q, use, h)
                    slot_work = ({2: first_ties}, {0: slots_before, 3: slot_ranks})[h] if ahead else {}
                    hidden(e, q, h, slot_work)
                if another:
                    for h in range(2):
                        turn_picked(e + 1, 1 - q, use + q, h)
                pe.wait_ge(s_w2[q], use * 16 + 16)
                if another:
                    down(e, q, 0)
                    down(e, q, 1)
                    back(e, 0, another)
                    back(e, 1, another)
                else:
                    for h in range(2):
                        down(e, q, h)
                        back(e, h, another)

            for q in range(2):
                expert(q, q, 0, True, True)
            with pe.Fori(1, E // 2 - 1) as pair:
                for q in range(2):
                    expert(pair * 2 + q, q, pair, True, True)
            for q in range(2):
                expert(E - 2 + q, q, E // 2 - 1, False, q == 0)

            pe.wait_ge(s_gelu, E * 2 * FT)
            pe.wait_ge(s_idx, E * 2)
            pe.wait_ge(s_yr, 2 * E)
            pe.wait_ge(s_yb, 4 * E)

            def turn_back(img, k, turn):
                pe.wait_ge(s_yl[k], turn * 16 + 16)
                if since(img, ENDS):
                    pe.wait_ge(s_fa, img - (ENDS - 1))
                for t in range(TPI):
                    ins = nc.tensor.transpose(end_regions[k][:, t // 4, (t % 4) * P:(t % 4 + 1) * P],
                                              y_in[k][:, t * C:(t + 1) * C], ident[0:P, 0:P])
                ins.then_inc(s_ft, 1)

            for k in range(ENDS):
                turn_back(k, k, 0)
            with pe.Fori(1, B // ENDS) as turn:
                for k in range(ENDS):
                    turn_back(turn * ENDS + k, k, turn)

        @block.vector
        def _(dve):
            def stats(region, st, s_math, img, s_turned):
                for a, tiles in enumerate(BANK_TILES):
                    dve.wait_ge(s_turned, img * 2 + a + 1)
                    for t in tiles:
                        ins = nc.vector.bn_stats(st[:, t, :], region[:, t, :])
                ins.then_inc(s_math, 1)

            def moments_a(st, sm, s_math, img):
                dve.wait_ge(s_math, img * 3 + 1)
                nc.vector.tensor_tensor(sm[:, 1, :], st[:, :, 1], st[:, :, 4], ALU.subtract)
                nc.vector.tensor_tensor(sm[:, 2, :], st[:, :, 2], st[:, :, 5], ALU.add)
                nc.vector.tensor_tensor(sm[:, 0, :], st[:, :, 1], st[:, :, 4], ALU.add).then_inc(s_math, 1)

            def moments_b(sm, s_math, img):
                dve.wait_ge(s_math, img * 3 + 2)
                nc.vector.scalar_tensor_tensor(sm[:, 1, :], sm[:, 1, :], C / 4.0, sm[:, 1, :], ALU.mult, ALU.mult)\
                    .then_inc(s_math, 1)

            def moments_c(sm, s_math, s_mom, img):
                dve.wait_ge(s_math, img * 3 + 3)
                nc.vector.tensor_tensor(sm[:, 3, :], sm[:, 1, :], sm[:, 2, :], ALU.add).then_inc(s_mom, 1)

            def inverse(sm, s_std, s_inv, img):
                dve.wait_ge(s_std, img + 1)
                nc.vector.reciprocal(sm[:, 5, :], sm[:, 4, :]).then_inc(s_inv, 1)

            def shift(sm, s_inv, s_sc, img):
                dve.wait_ge(s_inv, img + 1)
                nc.vector.scalar_tensor_tensor(sm[:, 6, :], sm[:, 0, :], -0.5, sm[:, 5, :], ALU.mult, ALU.mult)\
                    .then_inc(s_sc, 1)

            def tap(q, n, h, first):
                dy, dx = TAPS[PE_TAPS + n]
                y0, lines = (h * LINES, LINES) if first else (0, H)
                o = conv[:, q, y0 * W:(y0 + lines) * W].rearrange("c (h w) -> c h w", w=W)
                acc = psC[:, h, 0:HALF].rearrange("c (h w) -> c h w", w=W) if first else o
                return nc.vector.scalar_tensor_tensor(o, x_pad_v[:, q, y0 + dy:y0 + dy + lines, dx:dx + W],
                                                      taps_w[:, PE_TAPS + n:PE_TAPS + n + 1], acc, ALU.mult, ALU.add)

            def first_tap(img, q, h):
                dve.wait_ge(s_conv, img * 2 + h + 1)
                if since(img, 2):
                    dve.wait_ge(s_h1, img - 1)
                tap(q, 0, h, True).then_inc(s_taken, 1)

            def later_tap(img, q, n):
                if n == 1:
                    dve.wait_ge(s_taken, img * 2 + 2)
                else:
                    dve.wait_ge(s_tapn, img * (DVE_TAPS - 2) + n - 1)
                tap(q, n, 0, False).then_inc(s_tapn if n < DVE_TAPS - 1 else s_tap, 1)

            pv = prm[:, 0:8].rearrange("c (n k) -> c k n", k=4)

            def setup_first():
                dve.wait_ge(s_prm, 16 * 11)
                nc.vector.tensor_scalar(fold[:, 0:2], pv[:, 3, :], BN_EPS, None, ALU.add).then_inc(s_bnv, 1)
                nc.vector.tensor_tensor(fold[:, 6:8], prm[:, 8:10], pv[:, 2, :], ALU.subtract).then_inc(s_tiny, 1)

            def setup_rest():
                dve.wait_ge(s_bns, 1)
                nc.vector.reciprocal(fold[:, 10:12], fold[:, 2:4]).then_inc(s_tiny, 1)
                dve.wait_ge(s_tiny, 2)
                nc.vector.tensor_tensor(fold[:, 4:6], fold[:, 10:12], pv[:, 0, :], ALU.mult).then_inc(s_tiny, 1)
                dve.wait_ge(s_tiny, 3)
                nc.vector.tensor_tensor(fold[:, 8:10], fold[:, 6:8], fold[:, 4:6], ALU.mult).then_inc(s_tiny, 1)
                dve.wait_ge(s_tiny, 4)
                nc.vector.tensor_tensor(fold[:, 8:10], fold[:, 8:10], pv[:, 1, :], ALU.add)
                dve.wait_ge(s_const, 1)
                for n in range(PE_TAPS):
                    nc.vector.tensor_scalar(tap_diag[:, n, :], ident[:, :], taps_w[:, n:n + 1], None, ALU.mult)
                nc.vector.tensor_scalar(mod_i[:, :], mod_i[:, :], E - 1, None, ALU.bitwise_and).then_inc(s_tiny, 1)
                nc.vector.tensor_scalar(round_bits[:, :], round_bits[:, :], 29, None, ALU.logical_shift_left)
                nc.vector.tensor_scalar(part_i[:, 1:2], part_i[:, 0:1], B - 1, None, ALU.bitwise_and)
                nc.vector.tensor_scalar(part_i[:, 2:3], part_i[:, 0:1], 4, None, ALU.logical_shift_right).then_inc(s_tiny, 1)
                dve.wait_ge(s_tiny, 6)
                nc.vector.scalar_tensor_tensor(tile_col[:, :], part_i[:, 1:2], float(TPI), part_i[:, 2:3], ALU.mult, ALU.add)\
                    .then_inc(s_tiny, 1)
                dve.wait_ge(s_tiny, 7)
                nc.vector.tensor_scalar(before[:, :], tile_row[:, :], tile_col[:, :], None, ALU.is_gt)
                nc.vector.tensor_copy(s_abs[:, P:P + 1], tile_col[:, :])
                nc.vector.tensor_scalar(same_expert[:, :], mod_i[:, :], 0, None, ALU.is_equal)
                nc.vector.tensor_scalar(same16[:, :], mod_i[:, :], 0, None, ALU.is_equal)
                nc.vector.tensor_scalar(half_same[:, :], mod_i[:, :], 0, 0.5, ALU.is_equal, ALU.mult)
                dve.wait_ge(s_wps, 1)
                dve.wait_ge(s_wsb, 1)
                nc.vector.tensor_tensor(wr_c[:, :], wr_raw[:, :], psB[:, 0, 384:384 + E], ALU.subtract).then_inc(s_setup, 1)

            def step(pair, u):
                on0, img0, q0, _ = image(pair, u, 0)
                on1, img1, q1, _ = image(pair, u, 1)
                on2, img2, q2, _ = image(pair, u, 2)
                on3, img3, q3, use3 = image(pair, u, 3)
                on4, img4, q4, _ = image(pair, u, 4)
                on5, img5, q5, use5 = image(pair, u, 5)

                def keep_first():
                    dve.wait_ge(s_sg1, img3 + 1)
                    nc.vector.tensor_scalar(keep1[:, 1:2], keep1[:, 0:1], 0.5 - HW, None, ALU.is_gt).then_inc(s_kp1, 1)

                def mask_weights():
                    dve.wait_ge(s_kp1, img3 + 1)
                    if since(img3, 2):
                        dve.wait_ge(s_pw, img3 * 2 - 2)
                    if isinstance(img3, int) and img3 == 0:
                        dve.wait_ge(s_wsb, 1)
                    nc.vector.tensor_scalar(pw_masked[:, q3, :], pw_T[:, :], keep1[:, 1:2], None, ALU.mult).then_inc(s_wm, 1)

                if on0:
                    stats(ln_tiles, ln_st, s_m1, img0, s_t1)
                if on3 and not on1:
                    keep_first()
                    mask_weights()
                if on5:
                    if since(img5, 1):
                        dve.wait_ge(s_n3, img5)
                    inverse(row_sm, s_std3, s_inv3, img5)
                    dve.wait_ge(s_inv3, img5 + 1)
                    inv = row_sm[:, 5, :].unsqueeze(2).to_broadcast([P, TPI, E])
                    lg = logits[:, :].rearrange("p (t k) -> p t k", t=TPI)[:, :, ds(img5 * E, E)]
                    nc.vector.tensor_tensor(lg, logit_region(img5), inv, ALU.mult)
                    if since(img5, 2):
                        dve.wait_ge(s_rows[q5], use5 * 16)
                    nc.vector.tensor_tensor(rows[:, q5, :].rearrange("p (t c) -> p t c", c=ROW)[:, :, C:ROW],
                                            logit_region(img5), inv, ALU.mult).then_inc(s_rl, 1)
                if on3 and on1:
                    keep_first()
                if on5:
                    dve.wait_ge(s_rl, img5 + 1)
                    shift(row_sm, s_inv3, s_sc3, img5)
                if on2:
                    later_tap(img2, q2, 1)
                if on0:
                    moments_a(ln_st, ln_sm, s_m1, img0)
                if on3 and on1:
                    mask_weights()
                if on0:
                    moments_b(ln_sm, s_m1, img0)
                if on2:
                    later_tap(img2, q2, 2)
                if on0:
                    moments_c(ln_sm, s_m1, s_mom1, img0)
                    if isinstance(img0, int) and img0 == 0:
                        setup_first()
                if on2:
                    later_tap(img2, q2, 3)
                if on0:
                    inverse(ln_sm, s_std1, s_inv1, img0)
                if on2:
                    later_tap(img2, q2, 4)
                if on0:
                    shift(ln_sm, s_inv1, s_sc1, img0)
                    if isinstance(img0, int) and img0 == 0:
                        setup_rest()
                if on1:
                    first_tap(img1, q1, 0)
                if on3:
                    dve.wait_ge(s_sg2, img3 + 1)
                    nc.vector.tensor_scalar(keep2[:, 1:2], keep2[:, 0:1], 0.5 - HW, None, ALU.is_gt).then_inc(s_kp2, 1)
                    dve.wait_ge(s_kp2, img3 + 1)
                    dve.wait_ge(s_xres[q3], use3 * 16 + 16)
                    if since(img3, 2):
                        dve.wait_ge(s_t3, img3 * 2 - 2)
                        dve.wait_ge(s_x1c[q3], use3 * 16)
                    nc.vector.scalar_tensor_tensor(x1[:, q3, :], act2[:, q3, :], keep2[:, 1:2], x_res[:, q3, :],
                                                   ALU.mult, ALU.add).then_inc(s_x1, 1)
                if on4:
                    stats(row_region(img4), row_st, s_m3, img4, s_t3)
                    moments_a(row_st, row_sm, s_m3, img4)
                if on1:
                    first_tap(img1, q1, 1)
                if on4:
                    moments_b(row_sm, s_m3, img4)
                    moments_c(row_sm, s_m3, s_mom3, img4)

            steps(dve, step)

            la = psC[:, 0, 0:4 * P]
            lb = psC[:, 1, 0:3 * P]
            dve.wait_ge(s_sp, 1)
            nc.vector.reduce_max(bmax[:, 0:1], la, AX_X)
            nc.vector.reduce_max(bmax[:, 1:2], lb, AX_X).then_inc(s_sdi, 1)
            dve.wait_ge(s_sdi, 1)
            nc.vector.tensor_tensor(bmax[:, 0:1], bmax[:, 0:1], bmax[:, 1:2], ALU.max).then_inc(s_sd, 1)
            dve.wait_ge(s_sp, 2)
            nc.vector.tensor_reduce(mrow[:, 1, 0:E], psB[0:1, 0, 0:128].rearrange("a (i e) -> a e i", e=E), AX_X, ALU.max)\
                .then_inc(s_sdi, 1)
            dve.wait_ge(s_sdi, 2)
            nc.vector.tensor_copy(mrow[:, 2, :].rearrange("a (i e) -> a i e", e=E),
                                  mrow[:, 1, 0:E].unsqueeze(1).to_broadcast([1, B, E])).then_inc(s_sd, 1)
            dve.wait_ge(s_sp, 3)
            nc.vector.tensor_copy(mcol[:, :], psB[:, 0, 128:129]).then_inc(s_sdi, 1)
            dve.wait_ge(s_sdi, 3)
            nc.vector.tensor_scalar(dist[:, 0:4 * P], la, mcol[:, :], -1.0, ALU.subtract, ALU.mult)
            nc.vector.tensor_scalar(dist[:, 4 * P:HW], lb, mcol[:, :], -1.0, ALU.subtract, ALU.mult).then_inc(s_sd, 1)
            dve.wait_ge(s_sd, 3)
            nc.vector.tensor_scalar(odd_dist[:, :], dist[:, :].bitcast(I32), 1, None, ALU.bitwise_or).then_inc(s_odd, 1)

            def count(column, value, n, offset):
                return nc.vector.tensor_scalar(junk[:, column, 0:n], dist[:, 0:n], value.bitcast(F32), -offset, ALU.is_lt, ALU.add,
                                               accum_out=cnt[:, column:column + 1])

            def search_round(r, last):
                if last:
                    nc.vector.tensor_scalar(cand[:, 0:2], one_bit[:, :], prefix[:, :], None, ALU.bitwise_or).then_inc(s_cand, 1)
                else:
                    nc.vector.tensor_scalar(cand[:, :], round_bits[:, :], prefix[:, :], None, ALU.bitwise_or).then_inc(s_cand, 1)
                dve.wait_ge(s_cand, r * 3 + 1)
                ins = count(1, cand[:, 1:2], HW, OFFSET)
                if not last:
                    ins = count(2, cand[:, 2:3], HALF, OFFSET / 2)
                ins.then_inc(s_cnt, 1)
                if not last:
                    nc.vector.tensor_scalar(round_bits[:, :], round_bits[:, :], 2, None, ALU.logical_shift_right)
                n = 2 if last else 4
                dve.wait_ge(s_tot, r + 1)
                nc.vector.scalar_tensor_tensor(kept[:, 0:n], psA[:, 0, 0:n], LIMIT, cand[:, 0:n].bitcast(F32),
                                               ALU.is_lt, ALU.mult).then_inc(s_cand, 1)
                dve.wait_ge(s_cand, r * 3 + 2)
                nc.vector.reduce_max(prefix[:, :].bitcast(F32), kept[:, 0:n], AX_X).then_inc(s_cand, 1)
                dve.wait_ge(s_cand, r * 3 + 3)

            with dve.Fori(0, (ROUNDS - 1) // UNROLL) as turn:
                for k in range(UNROLL):
                    search_round(turn * UNROLL + k, False)
            search_round(ROUNDS - 1, True)
            count(1, prefix[:, :], HW, OFFSET).then_inc(s_cnt, 1)
            nc.vector.tensor_copy(tcol[:, 0:1], prefix[:, :].bitcast(F32)).then_inc(s_sd, 1)
            nc.vector.tensor_copy(tcol[:, 2:3], mcol[:, :]).then_inc(s_sd, 1)
            dve.wait_ge(s_sp, 4)
            nc.vector.reciprocal(tcol[:, 3:4], psB[:, 1, 0:1]).then_inc(s_sd, 1)
            dve.wait_ge(s_tot, ROUNDS + 1)
            nc.vector.tensor_scalar(tcol[:, 1:2], psA[:, 0, 1:2], -1.0, LIMIT, ALU.mult, ALU.add).then_inc(s_sd, 1)
            dve.wait_ge(s_sp, 5)
            nc.vector.tensor_copy(bc[:, :, :], psB[:, 0, :].rearrange("p (n k) -> p n k", n=4)[:, :, 0:E]).then_inc(s_sd, 1)
            dve.wait_ge(s_sd, 8)
            nc.vector.tensor_scalar(neg_max[:, :], bc[:, 2, :], -1.0, None, ALU.mult).then_inc(s_sd, 1)
            dve.wait_ge(s_ltc, 2)

            def col(n, e):
                return bc[0:P, n, ds(e, 1)]

            def slots_a(e):
                nc.vector.tensor_scalar(s_d[:, :], logits_T[:, ds(e * P, P)], col(2, e), -1.0, ALU.subtract, ALU.mult)\
                    .then_inc(s_pm, 1)
                dve.wait_ge(s_pm, e * PM + 1)
                nc.vector.tensor_scalar(s_eq[:, :], s_d[:, :], col(0, e), None, ALU.is_equal).then_inc(s_pm, 1)
                nc.vector.tensor_scalar(s_lt[:, :], s_d[:, :], col(0, e), None, ALU.is_lt)
                dve.wait_ge(s_pm, e * PM + 2)
                nc.vector.tensor_tensor_scan(s_eqr[:, :], ones[0:P, 0:P], s_eq[:, :], 0.0, ALU.mult, ALU.add).then_inc(s_pm, 1)

            def slots_b(e):
                dve.wait_ge(s_tie1, e + 1)
                nc.vector.tensor_tensor(s_lim[:, :], col(1, e), psD[0:P, 0, 120:121], ALU.subtract).then_inc(s_pm, 1)
                dve.wait_ge(s_pm, e * PM + 4)
                nc.vector.scalar_tensor_tensor(s_tie[:, :], s_eqr[:, :], s_lim[:, :], s_eq[:, :], ALU.is_le, ALU.mult)\
                    .then_inc(s_pm, 1)
                dve.wait_ge(s_pm, e * PM + 5)
                nc.vector.tensor_tensor(s_sel[:, :], s_tie[:, :], s_lt[:, :], ALU.add).then_inc(s_pm, 1)
                dve.wait_ge(s_pm, e * PM + 6)
                nc.vector.tensor_tensor_scan(s_rank[:, :], ones[0:P, 0:P], s_sel[:, :], 0.0, ALU.mult, ALU.add).then_inc(s_pm, 1)

            def slots_c(e):
                dve.wait_ge(s_cex, e + 1)
                nc.vector.tensor_copy(s_edge[:, 0:1], psD[0:P, 0, 121:122])
                nc.vector.tensor_tensor(s_edge[:, 1:2], s_rank[:, P - 1:P], psD[0:P, 0, 121:122], ALU.add).then_inc(s_pm, 1)
                dve.wait_ge(s_pm, e * PM + 8)
                nc.vector.tensor_scalar(s_abs[:, 0:P], s_rank[:, :], s_edge[:, 0:1], None, ALU.add)
                nc.vector.tensor_scalar(s_from[:, :], slot_row[:, :], s_edge[:, 0:1], None, ALU.is_ge)
                nc.vector.tensor_scalar(s_to[:, :], slot_row[:, :], s_edge[:, 1:2], None, ALU.is_lt).then_inc(s_pm, 1)
                dve.wait_ge(s_pm, e * PM + 9)
                nc.vector.tensor_tensor(s_in[:, :], s_from[:, :], s_to[:, :], ALU.mult).then_inc(s_own, 1)

            def slots_d(e, q, last_use):
                ranks = psD[:, :, :].rearrange("p a (b k) -> p (a b) k", k=128)
                if last_use is not None:
                    for h in range(2):
                        dve.wait_ge(s_gat[h][q], last_use * (8 * SB))
                for h in range(2):
                    blocks = slice(4 * h, 4 * h + 4)
                    dve.wait_ge(s_g, e * 2 + h + 1)
                    nc.vector.tensor_tensor(s_cmp[:, blocks, :], ranks[:, blocks, 0:P],
                                            slot_col[:, blocks].unsqueeze(2).to_broadcast([128, 4, P]), ALU.is_le).then_inc(s_pd, 1)
                    dve.wait_ge(s_pd, e * 4 + 2 * h + 1)
                    nc.vector.reduce_sum(s_p[:, blocks], s_cmp[:, blocks, :], AX_X).then_inc(s_pd, 1)
                    dve.wait_ge(s_pd, e * 4 + 2 * h + 2)
                    nc.vector.scalar_tensor_tensor(gather_idx[:, q, blocks], ranks[:, blocks, P], float(P), s_p[:, blocks],
                                                   ALU.mult, ALU.add).then_inc(s_idx, 1)

            for e in range(2):
                slots_a(e)
                slots_b(e)
                slots_c(e)
                slots_d(e, e, None)

            def bias_out(e, h):
                dve.wait_ge(s_l2, e * 2 + h + 1)
                if since(e, 1):
                    dve.wait_ge(s_bt, e * 2 - 1 + h)
                for part in range(2):
                    lo = part * HS // 2
                    nc.vector.tensor_scalar(y_T[:, h * HS + lo:h * HS + lo + HS // 2], psC[:, h, lo:lo + HS // 2],
                                            b2_T[:, ds(e, 1)], None, ALU.add).then_inc(s_yb, 1)

            def weigh(e, q, use, h):
                dve.wait_ge(s_gt, e + 1)
                dve.wait_ge(s_bt, e * 2 + h + 1)
                if since(e, 2):
                    dve.wait_ge(s_sca[q], use * (16 * SB))
                nc.vector.tensor_tensor(y_rows[:, q, 4 * h:4 * h + 4, :], psA[:, h, :].rearrange("s (b d) -> s b d", d=C),
                                        gate[:, 4 * h:4 * h + 4].unsqueeze(2).to_broadcast([128, 4, C]), ALU.mult).then_inc(s_yr, 1)

            def expert(e, q, use, ahead, last=False):
                if ahead:
                    slots_a(e + 2)
                    slots_b(e + 2)
                    slots_c(e + 2)
                if since(e, 2):
                    dve.wait_ge(s_sca[q], use * (16 * SB))
                nc.vector.tensor_copy(scatter_idx[:, q, :], gather_idx[:, q, :]).then_inc(s_si, 1)
                if ahead:
                    dve.wait_ge(s_si, e + 1)
                    slots_d(e + 2, q, use + 1)
                dve.wait_ge(s_ge, e + 1)
                if since(e, 1):
                    dve.wait_ge(s_yr, e * 2)
                nc.vector.tensor_scalar(gate[:, :], gate_e[:, :], bc[:, 3, ds(e, 1)], None, ALU.mult).then_inc(s_gt, 1)
                bias_out(e, 0)
                if last:
                    weigh(e, q, use, 0)
                bias_out(e, 1)
                if not last:
                    weigh(e, q, use, 0)
                weigh(e, q, use, 1)

            for q in range(2):
                expert(q, q, 0, True)
            with dve.Fori(1, E // 2 - 1) as pair:
                for q in range(2):
                    expert(pair * 2 + q, q, pair, True)
            for q in range(2):
                expert(E - 2 + q, q, E // 2 - 1, False, q == 1)

            for q in range(2):
                dve.wait_ge(s_x1c[q], 16 * B // 2)

            def add_up(img, k, turn):
                dve.wait_ge(s_ft, img + 1)
                if since(img, ENDS):
                    dve.wait_ge(s_fo[k], turn * 16)
                for a, (lo, n) in enumerate(((0, 4 * P), (4 * P, 3 * P))):
                    ins = nc.vector.tensor_tensor(o_img[k][:, 0, lo:lo + n], end_regions[k][:, a, 0:n],
                                                  x1_all[:, ds(img * HW + lo, n)], ALU.add)
                ins.then_inc(s_fa, 1)

            for k in range(ENDS):
                add_up(k, k, 0)
            with dve.Fori(1, B // ENDS) as turn:
                for k in range(ENDS):
                    add_up(turn * ENDS + k, k, turn)


_INS = ['x', 'L0_conv_dw_w', 'L0_conv_dw_b', 'L0_conv_bn1_g', 'L0_conv_bn1_b', 'L0_conv_bn1_m', 'L0_conv_bn1_v',
        'L0_conv_pw_w', 'L0_conv_pw_b', 'L0_conv_bn2_g', 'L0_conv_bn2_b', 'L0_conv_bn2_m', 'L0_conv_bn2_v',
        'L0_ffn_Wr', 'L0_ffn_W1', 'L0_ffn_b1', 'L0_ffn_W2', 'L0_ffn_b2']
_OUTS = [((B, C, H, W), 'float32')]


def kernel(**inputs):
    import numpy as _np
    import concourse.bacc as _bacc
    from concourse import mybir as _mybir
    from concourse.bass_utils import run_bass_kernel_spmd as _run

    nc = _bacc.Bacc("TRN2", target_bir_lowering=False, num_devices=1)
    arrays, args = {}, []
    for name in _INS:
        a = _np.ascontiguousarray(inputs[name])
        arrays[f"in_{name}_dram"] = a
        args.append(nc.dram_tensor(f"in_{name}_dram", a.shape, _mybir.dt.from_np(a.dtype), kind="ExternalInput").ap())
    for i, (shape, dtype) in enumerate(_OUTS):
        dt = _mybir.dt.from_np(_np.dtype(dtype))
        args.append(nc.dram_tensor(f"out_{i}_dram", shape, dt, kind="ExternalOutput").ap())
    build(nc, *args)
    r = _run(nc, [arrays], core_ids=[0])
    got = tuple(r.results[0][f"out_{i}_dram"] for i in range(len(_OUTS)))
    return got[0]
```
